# Optimizing a Trainium2 kernel written in Bass

```python
import numpy as np
import jax
import jax.numpy as jnp

def _softmax(x, axis=-1):
    return jax.nn.softmax(x, axis=axis)

def _gelu(x):
    return jax.nn.gelu(x, approximate=True)

def _silu(x):
    return jax.nn.silu(x)

def _sigmoid(x):
    return jax.nn.sigmoid(x)

def _layernorm(x, axis=-1, eps=1e-05):
    m = jnp.mean(x, axis=axis, keepdims=True)
    v = jnp.var(x, axis=axis, keepdims=True)
    return (x - m) / jnp.sqrt(v + eps)

def _scatter_add(tgt, idx, src, axis=0):
    return tgt.at[idx].add(src)

def _segment_sum(src, seg, n):
    return jax.ops.segment_sum(src, seg, n)
kernel_name = 'mk_adaln_attn_ffn_d1_seqx_r8_8e0554'

def setup_inputs(seed: int=0):
    np.random.seed(seed)
    _w = jnp.asarray

    def _rec_inputs():
        import jax
        import jax.numpy as jnp
        _rk = jax.random.key(seed)
        x = -0.000125 + 0.9999 * jax.random.normal(jax.random.fold_in(_rk, 1), (32, 32, 512), jnp.float32)
        _lenS = 32 - jax.random.randint(jax.random.fold_in(_rk, 7), (32,), 0, max(1, 32 // 4) + 1, jnp.int32)
        _lenS2 = 32 - jax.random.randint(jax.random.fold_in(_rk, 8), (32,), 0, max(1, 32 // 4) + 1, jnp.int32)
        cond_128 = 0.0061147 + 1.02565 * jax.random.normal(jax.random.fold_in(_rk, 11), (32, 128), jnp.float32)
        fside_S_0 = -0.022604 + 0.987366 * jax.random.normal(jax.random.fold_in(_rk, 12), (32,), jnp.float32)
        return (x, cond_128, fside_S_0)
    x, cond_128, fside_S_0 = _rec_inputs()

    def _L0_cond_setup():
        import jax, jax.numpy as jnp
        import numpy as np
        K = 8
        T = 1.0
        D_EMBD = 128
        IN_C = 32
        OUT_C = 32
        BS = 32
        H = 512
        HID = 128
        key = jax.random.key(seed)
        ks = jax.random.split(key, 10)
        s = lambda fan_in: 1.0 / np.sqrt(fan_in)
        return {'x': jax.random.normal(ks[0], (BS, IN_C, H), dtype=jnp.float32), 'embedding': jax.random.normal(ks[1], (BS, D_EMBD), dtype=jnp.float32), 'W0': jax.random.normal(ks[2], (D_EMBD, HID), dtype=jnp.float32) * s(D_EMBD), 'b0': jnp.zeros((HID,), dtype=jnp.float32), 'W1': jax.random.normal(ks[3], (HID, HID), dtype=jnp.float32) * s(HID), 'b1': jnp.zeros((HID,), dtype=jnp.float32), 'W2': jax.random.normal(ks[4], (HID, K), dtype=jnp.float32) * s(HID), 'b2': jnp.zeros((K,), dtype=jnp.float32), 'weight': jax.random.normal(ks[5], (K, OUT_C, IN_C, 1), dtype=jnp.float32) * s(IN_C), 'bias_k': jax.random.normal(ks[6], (K, OUT_C), dtype=jnp.float32) * 0.1}
    _L0_cond_all = _L0_cond_setup()
    _L0_cond_in = {k: v for k, v in _L0_cond_all.items() if k in ('W0', 'b0', 'W1', 'b1', 'W2', 'b2', 'weight', 'bias_k')}
    del _L0_cond_all

    def _L0_attn_setup():
        import math
        import jax, jax.numpy as jnp
        import numpy as np
        IN_F, OUT_F, HID = (512, 512, 512)
        WINDOW, STRIPES = (6, 3)

        def make_sparse_mask(n_in=IN_F, n_out=OUT_F, window=WINDOW, stripes=STRIPES):
            m = np.zeros((n_in, n_out), dtype=np.float32)
            stride = int(math.sqrt(n_in))
            for k in range(stripes):
                ps = stride * k
                for i in range(0, n_in, window):
                    m[ps + i:ps + i + window, i:i + window] = 1.0
            mb = m.astype(bool)
            return jnp.asarray((mb | mb.T).astype(np.float32))
        key = jax.random.key(seed)
        k1, k2, k3, k4 = jax.random.split(key, 4)
        scale = 1.0 / math.sqrt(IN_F)
        x = jax.random.normal(k1, (8, 96, IN_F), dtype=jnp.float32)
        w1 = jax.random.normal(k2, (HID, IN_F), dtype=jnp.float32) * scale
        w2 = jax.random.normal(k3, (OUT_F, HID), dtype=jnp.float32) * scale
        b2 = jax.random.normal(k4, (OUT_F,), dtype=jnp.float32) * scale
        return {'x': x, 'w1': w1, 'w2': w2, 'b2': b2, 'sparse_mask': make_sparse_mask()}
    _L0_attn_all = _L0_attn_setup()
    _L0_attn_in = {k: v for k, v in _L0_attn_all.items() if k in ('w1', 'w2', 'b2', 'sparse_mask')}
    del _L0_attn_all

    def _L0_cond2_setup():
        import jax, jax.numpy as jnp
        import numpy as np
        from jax import lax
        N, C_IN, L = (32, 32, 512)
        C_OUT, K, GROUPS = (32, 9, 4)
        C_DIM, PAD, STRIDE = (128, 4, 1)
        key = jax.random.key(seed)
        k1, k2, k3, k4, k5 = jax.random.split(key, 5)
        x = jax.random.normal(k1, (N, C_IN, L), dtype=jnp.float32)
        c = jax.random.normal(k2, (N, C_DIM), dtype=jnp.float32)
        weight = jax.random.normal(k3, (C_OUT, C_IN // GROUPS, K), dtype=jnp.float32)
        c_weight = jax.random.normal(k4, (C_OUT, C_DIM), dtype=jnp.float32)
        bias = jax.random.normal(k5, (C_OUT,), dtype=jnp.float32)
        return {'x': x, 'c': c, 'weight': weight, 'c_weight': c_weight, 'bias': bias}
    _L0_cond2_all = _L0_cond2_setup()
    _L0_cond2_in = {k: v for k, v in _L0_cond2_all.items() if k in ('weight', 'c_weight')}
    del _L0_cond2_all

    def _L0_ffn_setup():
        import jax, jax.numpy as jnp
        import numpy as np
        import math
        B, S, IN, OUT = (4, 256, 512, 512)
        E, R, K = (8, 64, 128)
        SCALE = 64.0 / 64.0
        MULTIPLIER = 1.0
        key = jax.random.key(seed)
        ks = jax.random.split(key, 6)
        return {'x': jax.random.normal(ks[0], (B, S, IN), jnp.float32), 'W_org': jax.random.normal(ks[1], (OUT, IN), jnp.float32) * 0.02, 'lora_down': jax.random.normal(ks[2], (E, IN, R), jnp.float32) * 0.02, 'lora_up': jax.random.normal(ks[3], (E, R, OUT), jnp.float32) * 0.02, 'lora_keys': jax.random.normal(ks[4], (E, K), jnp.float32), 'Wq': jax.random.normal(ks[5], (K, IN), jnp.float32) * 0.02}
    _L0_ffn_all = _L0_ffn_setup()
    _L0_ffn_in = {k: v for k, v in _L0_ffn_all.items() if k in ('W_org', 'lora_down', 'lora_up', 'lora_keys', 'Wq')}
    del _L0_ffn_all
    return {'x': x, 'cond_128': cond_128, 'fside_S_0': fside_S_0, 'L0_cond_W0': _L0_cond_in['W0'], 'L0_cond_b0': _L0_cond_in['b0'], 'L0_cond_W1': _L0_cond_in['W1'], 'L0_cond_b1': _L0_cond_in['b1'], 'L0_cond_W2': _L0_cond_in['W2'], 'L0_cond_b2': _L0_cond_in['b2'], 'L0_cond_weight': _L0_cond_in['weight'], 'L0_cond_bias_k': _L0_cond_in['bias_k'], 'L0_attn_w1': _L0_attn_in['w1'], 'L0_attn_w2': _L0_attn_in['w2'], 'L0_attn_b2': _L0_attn_in['b2'], 'L0_attn_sparse_mask': _L0_attn_in['sparse_mask'], 'L0_cond2_weight': _L0_cond2_in['weight'], 'L0_cond2_c_weight': _L0_cond2_in['c_weight'], 'L0_ffn_W_org': _L0_ffn_in['W_org'], 'L0_ffn_lora_down': _L0_ffn_in['lora_down'], 'L0_ffn_lora_up': _L0_ffn_in['lora_up'], 'L0_ffn_lora_keys': _L0_ffn_in['lora_keys'], 'L0_ffn_Wq': _L0_ffn_in['Wq']}

def reference(x, cond_128, fside_S_0, L0_cond_W0, L0_cond_b0, L0_cond_W1, L0_cond_b1, L0_cond_W2, L0_cond_b2, L0_cond_weight, L0_cond_bias_k, L0_attn_w1, L0_attn_w2, L0_attn_b2, L0_attn_sparse_mask, L0_cond2_weight, L0_cond2_c_weight, L0_ffn_W_org, L0_ffn_lora_down, L0_ffn_lora_up, L0_ffn_lora_keys, L0_ffn_Wq):
    import jax
    import jax.numpy as jnp

    def _L0_cond_ref(x, embedding, W0, b0, W1, b1, W2, b2, weight, bias_k):
        import jax, jax.numpy as jnp
        import numpy as np
        K = 8
        T = 1.0
        D_EMBD = 128
        IN_C = 32
        OUT_C = 32
        BS = 32
        H = 512
        HID = 128
        h = jax.nn.gelu(embedding @ W0 + b0, approximate=False)
        h = jax.nn.gelu(h @ W1 + b1, approximate=False)
        att = jax.nn.softmax((h @ W2 + b2) / T, axis=-1)
        agg_w = jnp.einsum('bk,koi->boi', att, weight[..., 0])
        agg_b = att @ bias_k
        out = jnp.einsum('boi,bih->boh', agg_w, x) + agg_b[:, :, None]
        return out

    def _L0_attn_ref(x, w1, w2, b2, sparse_mask):
        import math
        import jax, jax.numpy as jnp
        import numpy as np
        IN_F, OUT_F, HID = (512, 512, 512)
        WINDOW, STRIPES = (6, 3)

        def make_sparse_mask(n_in=IN_F, n_out=OUT_F, window=WINDOW, stripes=STRIPES):
            m = np.zeros((n_in, n_out), dtype=np.float32)
            stride = int(math.sqrt(n_in))
            for k in range(stripes):
                ps = stride * k
                for i in range(0, n_in, window):
                    m[ps + i:ps + i + window, i:i + window] = 1.0
            mb = m.astype(bool)
            return jnp.asarray((mb | mb.T).astype(np.float32))
        attn = jnp.einsum('ds,td->st', w1, w2) * sparse_mask
        y = jnp.einsum('bds,st->bdt', x, attn) + b2
        return jax.nn.gelu(y, approximate=False)

    def _L0_cond2_ref(x, c, weight, c_weight, bias):
        import jax, jax.numpy as jnp
        import numpy as np
        from jax import lax
        N, C_IN, L = (32, 32, 512)
        C_OUT, K, GROUPS = (32, 9, 4)
        C_DIM, PAD, STRIDE = (128, 4, 1)
        out = lax.conv_general_dilated(x, weight, window_strides=(STRIDE,), padding=[(PAD, PAD)], dimension_numbers=('NCH', 'OIH', 'NCH'), feature_group_count=GROUPS)
        ctx = jnp.einsum('nd,od->no', c, c_weight)
        out = out + ctx[:, :, None] + bias[None, :, None]
        return out

    def _L0_ffn_ref(x, W_org, lora_down, lora_up, lora_keys, Wq):
        import jax, jax.numpy as jnp
        import numpy as np
        import math
        B, S, IN, OUT = (4, 256, 512, 512)
        E, R, K = (8, 64, 128)
        SCALE = 64.0 / 64.0
        MULTIPLIER = 1.0
        base = jnp.einsum('bsi,oi->bso', x, W_org)
        q = jnp.einsum('bi,ki->bk', x.mean(axis=1), Wq)
        scores = jnp.einsum('bk,ek->be', q, lora_keys) / math.sqrt(K)
        coeffs = jax.nn.softmax(scores, axis=-1)
        h = jnp.einsum('bsi,eir->bser', x, lora_down)
        delta = jnp.einsum('be,bser,ero->bso', coeffs, h, lora_up)
        return base + delta * (SCALE * MULTIPLIER)
    x = x + _L0_attn_ref(_L0_cond_ref(x, cond_128, L0_cond_W0, L0_cond_b0, L0_cond_W1, L0_cond_b1, L0_cond_W2, L0_cond_b2, L0_cond_weight, L0_cond_bias_k), L0_attn_w1, L0_attn_w2, L0_attn_b2, L0_attn_sparse_mask)
    x = x + _L0_ffn_ref(_L0_cond2_ref(x, cond_128, L0_cond2_weight, L0_cond2_c_weight, fside_S_0), L0_ffn_W_org, L0_ffn_lora_down, L0_ffn_lora_up, L0_ffn_lora_keys, L0_ffn_Wq)
    return x

_drawn_inputs = setup_inputs


def setup_inputs(seed=0):
    import zlib

    import numpy as np

    out = dict(_drawn_inputs(seed))
    spreads = {'L0_cond_b0': (0.0, 0.8), 'L0_cond_b1': (0.0, 0.8), 'L0_cond_b2': (0.0, 0.8)}
    factors = {'L0_cond_W0': 6.85,
     'L0_cond_W1': 6.385,
     'L0_cond_W2': 5.921,
     'L0_cond_bias_k': 8.0,
     'L0_attn_b2': 4.471}
    for name, (base, spread) in spreads.items():
        noise = np.random.default_rng([zlib.crc32(name.encode()), seed]).standard_normal(out[name].shape)
        drawn = base * np.exp(spread * noise) if base else spread * noise
        out[name] = jnp.asarray(drawn.astype(out[name].dtype))
    for name, factor in factors.items():
        out[name] = (out[name] * factor).astype(out[name].dtype)
    return out
```

```python
from contextlib import ExitStack

import concourse.bass as bass
from concourse import mybir

ALU = mybir.AluOpType
ACT = mybir.ActivationFunctionType
AX = mybir.AxisListType
F32 = mybir.dt.float32
F32R = mybir.dt.float32r

P = 128
B, C, L = 32, 32, 512
NT = B * C // P
BT = P // C
Q = L // P
M = L // Q
KC, TAPS, GROUPS, PAD = 8, 9, 4, 4
E, R = 8, 64
HID = 128
TG = 2
NG = NT // TG
NH = NT // 2
BG = TG * BT
NTG = TG * P
ROUTER_SCALE = 1.0 / (C * float(P) ** 0.5)

_PACK = [("emb_t", B), ("w0", HID), ("b0", 1), ("w1", HID), ("b1", 1), ("w2", KC), ("b2", KC),
         ("keys_t", E), ("ctx_w_t", C), ("ctx_bias", C), ("bias_k", C)]
_CONST = [("eye", B), ("batch_rows", P), ("batch_tile", NT), ("own_block", BT)]


def columns(parts):
    at, out = 0, {}
    for name, n in parts:
        out[name] = (at, at + n)
        at += n
    return out, at


PACK, PACK_N = columns(_PACK)
CONST, CONST_N = columns(_CONST)


def adaln_attn_ffn(nc, x, small, const, kernels_k, attn_w1, attn_w2t, mask, attn_b2, wq, conv_w,
                   ffn_w, lora_down, lora_up, out):
    with ExitStack() as ctx:
        def sb(name, shape, dt=F32):
            return ctx.enter_context(nc.sbuf_tensor(name, shape, dt))

        def sem(name):
            return ctx.enter_context(nc.semaphore(name))

        small_sb = sb("small_sb", [P, PACK_N])
        const_sb = sb("const_sb", [P, CONST_N])
        ones = sb("ones", [P, P])
        table_dummy = sb("table_dummy", [1, 3])
        kernels_sb = sb("kernels_sb", [P, C, KC])
        wq_sb = sb("wq_sb", [P, L])
        conv_sb = sb("conv_sb", [P, 3, P])
        b2_sb = sb("b2_sb", [P, L])
        w1_raw = sb("w1_raw", [P, Q, L])
        w2_raw = sb("w2_raw", [P, Q, L])
        w1_hi = sb("w1_hi", [P, Q, L], F32R)
        w1_lo = sb("w1_lo", [P, Q, L], F32R)
        w2_hi = sb("w2_hi", [P, Q, L], F32R)
        w2_lo = sb("w2_lo", [P, Q, L], F32R)
        mask_sb = sb("mask_sb", [P, Q, L])
        s32 = sb("s32", [P, 2, L])
        s_hi = sb("s_hi", [P, Q, L], F32R)
        s_lo = sb("s_lo", [P, Q, L], F32R)
        x_slot = sb("x_slot", [P, 2, L])
        x1 = sb("x1", [P, NT, L])
        cond32 = sb("cond32", [P, 2, Q, P])
        cond_hi_sb = sb("cond_hi_sb", [P, 2, Q, P], F32R)
        cond_lo_sb = sb("cond_lo_sb", [P, 2, Q, P], F32R)
        y_gelu = sb("y_gelu", [P, 4, L])
        y32, gelu_sb = y_gelu[:, 0:2, :], y_gelu[:, 2:4, :]
        down_hi = sb("down_hi", [P, Q, L], F32R)
        down_lo = sb("down_lo", [P, Q, L], F32R)
        ffn_hi = sb("ffn_hi", [P, Q, L], F32R)
        ffn_lo = sb("ffn_lo", [P, Q, L], F32R)
        up_hi = sb("up_hi", [P, Q, L], F32R)
        up_lo = sb("up_lo", [P, Q, L], F32R)
        poly = sb("poly", [P, BG, M + 2])
        mix = sb("mix", [P, NT, BT, C])
        mix_rows = sb("mix_rows", [P, NT, C])
        mix_bias = sb("mix_bias", [P, NT, P])
        ctx_rows = sb("ctx_rows", [P, NT, P])
        att_rows = sb("att_rows", [P, NT, KC])
        folded_keys = sb("folded_keys", [P, Q, E])
        h1 = sb("h1", [P, B])
        h2 = sb("h2", [P, B])
        logits = sb("logits", [B, KC])
        att_max = sb("att_max", [B, 1])
        att_exp = sb("att_exp", [B, KC])
        att_sum = sb("att_sum", [B, 1])
        att_inv = sb("att_inv", [B, 1])
        att = sb("att", [B, KC])
        att_tiles = sb("att_tiles", [B, NT, KC])
        att_t = sb("att_t", [KC, B])
        zsum = sb("zsum", [P, Q, BG])
        router_max = sb("router_max", [BG, 1])
        router_bias = sb("router_bias", [BG, 1])
        router_exp = sb("router_exp", [BG, E])
        router_sum = sb("router_sum", [BG, 1])
        router_inv = sb("router_inv", [BG, 1])
        coef = sb("coef", [BG, E, R])
        coef_rows = sb("coef_rows", [P, Q, BG])
        mix_prod = y_gelu[:, :, :].rearrange("p a b -> p (a b)").rearrange("p (t o k) -> p t o k", t=NT, k=KC)
        down_raw, ffn_raw, up_raw = w1_raw, w2_raw, w1_raw
        z32 = mask_sb[:, 0:2, :].rearrange("p a b -> p (a b)").rearrange("p (q n) -> p q n", q=Q)
        h32 = mask_sb[:, 2:4, :].rearrange("p a b -> p (a b)").rearrange("p (q n) -> p q n", q=Q)

        def operand(t):
            return t[:, 0:2, :].rearrange("p a b -> p (a b)").rearrange("p (q n) -> p q n", q=Q)

        z_hi_sb, z_lo_sb, h_hi_sb, h_lo_sb = map(operand, (w1_hi, w1_lo, w2_hi, w2_lo))

        def part(name, rows=P):
            a, b = PACK[name]
            return small_sb[0:rows, a:b]

        def cpart(name, rows=P):
            a, b = CONST[name]
            return const_sb[0:rows, a:b]

        bank = [ctx.enter_context(nc.psum_tensor(f"bank{i}", [P, L], F32)) for i in range(8)]
        s_ps = bank[0:4]
        y_ps, out_ps = bank[0:2], bank[0:2]
        z_ps = bank[2:4]
        ctx_ps, cond_ps, h_ps = bank[4:6], bank[4:6], bank[4:6]
        bias_ps = bank[6:8]
        mlp_ps = router_ps = bank[6]
        h1_ps, h2_ps, logits_ps = mlp_ps[:, 0:B], mlp_ps[:, B:2 * B], mlp_ps[0:B, 2 * B:2 * B + KC]
        att_t_ps, att_rows_ps = mlp_ps[0:KC, 96:96 + B], mlp_ps[:, 128:128 + NT * KC]
        keys_ps = coef_ps = bank[7][:, 0:Q * E]

        small_in, const_in, kernels_in, wq_in = sem("small_in"), sem("const_in"), sem("kernels_in"), sem("wq_in")
        conv_in, b2_in, mask_in, x1_in = sem("conv_in"), sem("b2_in"), sem("mask_in"), sem("x1_in")
        w1_in = [sem(f"w1_in{d}") for d in range(Q)]
        w2_in = [sem(f"w2_in{d}") for d in range(Q)]
        down_in, ffn_in, up_in = sem("down_in"), sem("ffn_in"), sem("up_in")
        x_slot_in = [sem(f"x_slot_in{u}") for u in range(2)]
        w1_hi_ok, w1_lo_ok = sem("w1_hi_ok"), sem("w1_lo_ok")
        w2_hi_ok, w2_lo_ok = sem("w2_hi_ok"), sem("w2_lo_ok")
        ones_ok, zeros_ok = sem("ones_ok"), sem("zeros_ok")
        mlp_mm = sem("mlp_mm")
        gelus = sem("gelus")
        soft = sem("soft")
        att_exp_ok, att_mm = sem("att_exp_ok"), sem("att_mm")
        bias_terms, bias_mm, ctx_terms, ctx_mm = sem("bias_terms"), sem("bias_mm"), sem("ctx_terms"), sem("ctx_mm")
        ctx_ok, bias_ok, keys_mm, keys_ok, mix_ok = sem("ctx_ok"), sem("bias_ok"), sem("keys_mm"), sem("keys_ok"), sem("mix_ok")
        mix_step, mix_sums = sem("mix_step"), sem("mix_sums")
        s_mm, s_hi_ok, s_lo_ok = sem("s_mm"), sem("s_hi_ok"), sem("s_lo_ok")
        s_then_y = sem("s_then_y")
        split_hi, down_ok, ffn_ok, up_ok = sem("split_hi"), sem("down_ok"), sem("ffn_ok"), sem("up_ok")
        cond_mm, cond_biased, cond_hi, cond_lo = sem("cond_mm"), sem("cond_biased"), sem("cond_hi"), sem("cond_lo")
        y_mm = sem("y_mm")
        mix_then_x1 = sem("mix_then_x1")
        poly_in, conv_mm, z_ok, z_hi, z_lo = sem("poly_in"), sem("conv_mm"), sem("z_ok"), sem("z_hi"), sem("z_lo")
        zsum_ok, router_mm, router_step, router_exp_ok = sem("zsum_ok"), sem("router_mm"), sem("router_step"), sem("router_exp_ok")
        coef_ok, coef_mm, coef_rows_ok = sem("coef_ok"), sem("coef_mm"), sem("coef_rows_ok")
        h_mm, h_ok, h_hi, h_lo = sem("h_mm"), sem("h_ok"), sem("h_hi"), sem("h_lo")
        base_mm, out_mm, out_ok, out_stored = sem("base_mm"), sem("out_mm"), sem("out_ok"), sem("out_stored")

        block = ctx.enter_context(nc.Block())

        @block.sync
        def _(sp):
            sp.dma_start(small_sb[:, :], small).then_inc(small_in, 16)
            for d in range(Q):
                sp.dma_start(w1_raw[:, d, :], attn_w1[d]).then_inc(w1_in[d], 16)
                sp.dma_start(w2_raw[:, d, :], attn_w2t[d]).then_inc(w2_in[d], 16)
                if d == 1:
                    sp.dma_start(const_sb[:, :], const).then_inc(const_in, 16)
                    sp.dma_start(kernels_sb[:, :, :], kernels_k).then_inc(kernels_in, 16)
            sp.dma_start(mask_sb[:, :, :], mask).then_inc(mask_in, 16)
            for u in range(2):
                sp.dma_start(x_slot[:, u, :], x[u]).then_inc(x_slot_in[u], 16)
            sp.dma_start(b2_sb[:, :], attn_b2).then_inc(b2_in, 16)
            sp.dma_start(wq_sb[:, :], wq).then_inc(wq_in, 16)
            sp.dma_start(x1[:, :, :], x.rearrange("t p l -> p t l")).then_inc(x1_in, 16)
            sp.dma_start(conv_sb[:, :, :], conv_w).then_inc(conv_in, 16)

            def load_slot(t, u):
                sp.wait_ge(cond_mm, t - 1)
                sp.dma_start(x_slot[:, u, :], x[bass.ds(t, 1)].rearrange("t p l -> (t p) l")).then_inc(x_slot_in[u], 16)

            with sp.Fori(1, NT // 2) as q:
                load_slot(q * 2, 0)
                load_slot(q * 2 + 1, 1)

            def regroup(g):
                sp.wait_ge(mix_then_x1, g * TG + TG + 1)
                for u in range(TG):
                    for b in range(BT):
                        sp.dma_start(poly[:, u * BT + b, 1:M + 1],
                                     x1[C * b:C * (b + 1), bass.ds(g * TG + u, 1), :].rearrange("i t (r m) -> i (t r) m", r=Q)
                                     ).then_inc(poly_in, 16)

            def store(t):
                sp.wait_ge(out_ok, t + 1)
                sp.dma_start(out[bass.ds(t, 1)].rearrange("t p l -> (t p) l"), x1[:, bass.ds(t, 1), :].rearrange("p t l -> p (t l)")).then_inc(out_stored, 16)

            sp.wait_ge(zeros_ok, 2)
            regroup(0)
            sp.wait_ge(conv_mm, TG)
            regroup(1)
            with sp.Fori(1, NG - 1) as g:
                sp.wait_ge(conv_mm, g * TG + TG)
                regroup(g + 1)
                store(g * TG - TG)
                store(g * TG - TG + 1)
            for t in range(NT - 2 * TG, NT):
                store(t)
            sp.wait_ge(out_stored, 16 * NT)

        @block.gpsimd
        def _(pool):
            nc.gpsimd.memset(ones[:, :], 1.0).then_inc(ones_ok, 1)
            nc.gpsimd.memset(poly[:, :, 0:1], 0.0).then_inc(zeros_ok, 1)
            nc.gpsimd.memset(poly[:, :, M + 1:M + 2], 0.0).then_inc(zeros_ok, 1)
            for d in range(Q):
                pool.wait_ge(w2_hi_ok, d + 1)
                nc.gpsimd.tensor_tensor(w2_lo[:, d, :], w2_raw[:, d, :], w2_hi[:, d, :].bitcast(F32), ALU.subtract).then_inc(w2_lo_ok, 1)

            def split(raw, hi, lo, done, before):
                for d in range(Q):
                    nc.gpsimd.tensor_copy(hi[:, d, :], raw[:, d, :]).then_inc(split_hi, 1)
                    pool.wait_ge(split_hi, before + d + 1)
                    nc.gpsimd.tensor_tensor(lo[:, d, :], raw[:, d, :], hi[:, d, :].bitcast(F32), ALU.subtract).then_inc(done, 1)

            pool.wait_ge(mix_step, 1)
            pool.wait_ge(kernels_in, 16)
            pool.wait_ge(const_in, 16)
            nc.gpsimd.tensor_tensor(mix_prod[:, NH:NT], att_rows[:, NH:NT, :].unsqueeze(2).broadcast_to([P, NH, C, KC]),
                                    kernels_sb[:, :, :].unsqueeze(1).broadcast_to([P, NH, C, KC]),
                                    ALU.mult).then_inc(mix_sums, 1)
            n, left = 1, KC // 2
            while left:
                pool.wait_ge(mix_sums, n)
                sums = mix_prod[:, NH:NT, :, 0:left] if left > 1 else mix_rows[:, NH:NT, :].unsqueeze(3)
                nc.gpsimd.tensor_tensor(sums, mix_prod[:, NH:NT, :, 0:left], mix_prod[:, NH:NT, :, left:2 * left],
                                        ALU.add).then_inc(mix_sums, 1)
                n, left = n + 1, left // 2
            pool.wait_ge(mix_sums, n)
            nc.gpsimd.tensor_tensor(mix[:, NH:NT], mix_rows[:, NH:NT, :].unsqueeze(2).broadcast_to([P, NH, BT, C]),
                                    cpart("own_block").unsqueeze(1).unsqueeze(3).broadcast_to([P, NH, BT, C]),
                                    ALU.mult).then_inc(mix_then_x1, 1)

            pool.wait_ge(w1_hi_ok, Q)
            pool.wait_ge(w1_lo_ok, Q)
            pool.dma_start(down_raw[:, :, :], lora_down).then_inc(down_in, 16)
            pool.wait_ge(down_in, 16)
            pool.wait_ge(w2_hi_ok, Q)
            pool.wait_ge(w2_lo_ok, Q)
            pool.dma_start(ffn_raw[:, :, :], ffn_w).then_inc(ffn_in, 16)
            split(down_raw, down_hi, down_lo, down_ok, 0)
            pool.wait_ge(down_ok, Q)
            pool.dma_start(up_raw[:, :, :], lora_up).then_inc(up_in, 16)
            pool.wait_ge(ffn_in, 16)
            split(ffn_raw, ffn_hi, ffn_lo, ffn_ok, Q)
            pool.wait_ge(up_in, 16)
            split(up_raw, up_hi, up_lo, up_ok, 2 * Q)

        @block.scalar
        def _(act):
            def load_table(func, n):
                nc.scalar.activation(table_dummy[:, n:n + 1], ones[0:1, 0:1], func)

            act.wait_ge(ones_ok, 1)
            load_table(ACT.Gelu, 0)

            def w1_part(d):
                act.wait_ge(w1_in[d], 16)
                nc.scalar.copy(w1_hi[:, d, :], w1_raw[:, d, :]).then_inc(w1_hi_ok, 1)

            act.wait_ge(small_in, 16)
            act.wait_ge(mlp_mm, 1)
            nc.scalar.activation(h1[:, :], h1_ps, ACT.Gelu, bias=part("b0")).then_inc(gelus, 1)
            w1_part(0)
            act.wait_ge(mlp_mm, 2)
            nc.scalar.activation(h2[:, :], h2_ps, ACT.Gelu, bias=part("b1")).then_inc(gelus, 1)
            w1_part(1)
            load_table(ACT.Exp, 1)
            w1_part(2)
            act.wait_ge(soft, 3)
            nc.scalar.activation(att_exp[:, :], logits[:, :], ACT.Exp, accum_out=att_sum[:, :]).then_inc(att_exp_ok, 1)
            w1_part(3)
            load_table(ACT.Gelu, 2)
            def hi_of_s(q):
                act.wait_ge(s_then_y, q + 1)
                nc.scalar.copy(s_hi[:, q, :], s32[:, q % 2, :]).then_inc(s_hi_ok, 1)

            def hi_of_cond(t, u, slot_used):
                act.wait_ge(cond_biased, t + 1)
                if slot_used:
                    act.wait_ge(y_mm, t - 1)
                nc.scalar.copy(cond_hi_sb[:, u], cond32[:, u]).then_inc(cond_hi, 1)

            def gelu(t, u, used):
                act.wait_ge(s_then_y, t + Q + 1)
                act.wait_ge(mix_then_x1, used)
                nc.scalar.activation(gelu_sb[:, u, :], y32[:, u, :], ACT.Gelu).then_inc(gelus, 1)

            hi_of_s(0)
            hi_of_s(1)
            hi_of_cond(0, 0, False)
            hi_of_cond(1, 1, False)
            hi_of_s(2)
            hi_of_s(3)
            gelu(0, 0, 1)
            with act.Fori(0, NT // 2 - 1) as q:
                for k, u in ((q * 2 + 1, 1), (q * 2 + 2, 0)):
                    hi_of_cond(k + 1, 1 - u, True)
                    gelu(k, u, k)

            def hi_of_z(g, slot_used):
                act.wait_ge(z_ok, g * TG + TG)
                if slot_used:
                    act.wait_ge(base_mm, g)
                nc.scalar.copy(z_hi_sb, z32).then_inc(z_hi, 1)

            def router_exps(g):
                act.wait_ge(router_step, g * 3 + 2)
                nc.scalar.activation(router_exp[:, :], router_ps[0:BG, 0:E], ACT.Exp, bias=router_bias[:, :],
                                     scale=ROUTER_SCALE, accum_out=router_sum[:, :]).then_inc(router_exp_ok, 1)

            def hi_of_h(g, slot_used):
                if slot_used:
                    act.wait_ge(out_mm, g * TG)
                for v in range(2):
                    act.wait_ge(h_ok, g * 2 + v + 1)
                    nc.scalar.copy(h_hi_sb[:, 2 * v:2 * v + 2], h32[:, 2 * v:2 * v + 2]).then_inc(h_hi, 1)

            hi_of_z(0, False)
            gelu(NT - 1, 1, NT - 1)
            router_exps(0)
            hi_of_h(0, False)
            with act.Fori(1, NG) as g:
                hi_of_z(g, True)
                router_exps(g)
                hi_of_h(g, True)

        @block.vector
        def _(dve):
            def w_parts(d):
                dve.wait_ge(w2_in[d], 16)
                nc.vector.tensor_copy(w2_hi[:, d, :], w2_raw[:, d, :]).then_inc(w2_hi_ok, 1)
                dve.wait_ge(w1_hi_ok, d + 1)
                nc.vector.tensor_tensor(w1_lo[:, d, :], w1_raw[:, d, :], w1_hi[:, d, :].bitcast(F32),
                                        ALU.subtract).then_inc(w1_lo_ok, 1)

            dve.wait_ge(small_in, 16)
            nc.vector.tensor_tensor(ctx_rows[:, :, :].rearrange("p t (b o) -> p (t b) o", o=C),
                                    part("emb_t").unsqueeze(2).broadcast_to([P, B, C]),
                                    part("ctx_w_t").unsqueeze(1).broadcast_to([P, B, C]), ALU.mult).then_inc(ctx_terms, 1)
            w_parts(0)
            w_parts(1)
            dve.wait_ge(mlp_mm, 3)
            nc.vector.tensor_tensor(logits[:, :], logits_ps, part("b2", B), ALU.add).then_inc(soft, 1)
            dve.wait_ge(soft, 1)
            nc.vector.tensor_reduce(att_max[:, :], logits[:, :], AX.X, ALU.max).then_inc(soft, 1)
            dve.wait_ge(soft, 2)
            nc.vector.tensor_scalar(logits[:, :], logits[:, :], att_max[:, 0:1], None, ALU.subtract).then_inc(soft, 1)
            dve.wait_ge(ctx_mm, 1)
            for v in range(2):
                nc.vector.tensor_tensor(ctx_rows[:, v * NT // 2:(v + 1) * NT // 2, :].rearrange("p t (b o) -> p (t b) o", o=C),
                                        ctx_ps[v][:, :].rearrange("p (b o) -> p b o", o=C),
                                        part("ctx_bias").unsqueeze(1).broadcast_to([P, B // 2, C]), ALU.add).then_inc(ctx_ok, 1)
            w_parts(2)
            dve.wait_ge(att_exp_ok, 1)
            nc.vector.reciprocal(att_inv[:, :], att_sum[:, :]).then_inc(soft, 1)
            dve.wait_ge(soft, 4)
            nc.vector.tensor_scalar(att[:, :], att_exp[:, :], att_inv[:, 0:1], None, ALU.mult).then_inc(soft, 1)
            dve.wait_ge(soft, 5)
            dve.wait_ge(const_in, 16)
            nc.vector.tensor_tensor(att_tiles[:, :, :], att[:, :].unsqueeze(1).broadcast_to([B, NT, KC]),
                                    cpart("batch_tile", B).unsqueeze(2).broadcast_to([B, NT, KC]),
                                    ALU.mult).then_inc(soft, 1)
            w_parts(3)
            dve.wait_ge(att_mm, 1)
            nc.vector.tensor_copy(att_t[:, :], att_t_ps).then_inc(soft, 1)
            dve.wait_ge(soft, 7)
            nc.vector.tensor_tensor(mix_bias[0:KC].rearrange("k t (b o) -> k (t b) o", o=C),
                                    att_t[:, :].unsqueeze(2).broadcast_to([KC, B, C]),
                                    part("bias_k", KC).unsqueeze(1).broadcast_to([KC, B, C]),
                                    ALU.mult).then_inc(bias_terms, 1)
            nc.vector.tensor_copy(att_rows[:, :, :], att_rows_ps.rearrange("p (t k) -> p t k", t=NT)).then_inc(mix_step, 1)
            dve.wait_ge(mix_step, 1)
            dve.wait_ge(kernels_in, 16)

            nc.vector.tensor_tensor(mix_prod[:, 0:NH], att_rows[:, 0:NH, :].unsqueeze(2).broadcast_to([P, NH, C, KC]),
                                    kernels_sb[:, :, :].unsqueeze(1).broadcast_to([P, NH, C, KC]),
                                    ALU.mult).then_inc(mix_step, 1)
            dve.wait_ge(mix_step, 2)
            nc.vector.tensor_reduce(mix_rows[:, 0:NH, :], mix_prod[:, 0:NH], AX.X, ALU.add).then_inc(mix_step, 1)
            dve.wait_ge(mix_step, 3)
            nc.vector.tensor_tensor(mix[:, 0:NH], mix_rows[:, 0:NH, :].unsqueeze(2).broadcast_to([P, NH, BT, C]),
                                    cpart("own_block").unsqueeze(1).unsqueeze(3).broadcast_to([P, NH, BT, C]),
                                    ALU.mult).then_inc(mix_ok, 1)

            def bias_cond(t, u, slot_used):
                dve.wait_ge(cond_mm, t + 1)
                if slot_used:
                    dve.wait_ge(cond_hi, t - 1)
                bias = mix_bias[:, bass.ds(t, 1), :].broadcast_to([P, Q, P])
                nc.vector.tensor_tensor(cond32[:, u], cond_ps[u][:, :].rearrange("p (q n) -> p q n", q=Q),
                                        bias, ALU.add).then_inc(cond_biased, 1)

            def lo_of_cond(t, u, slot_used):
                dve.wait_ge(cond_hi, t + 1)
                if slot_used:
                    dve.wait_ge(y_mm, t - 1)
                nc.vector.tensor_tensor(cond_lo_sb[:, u], cond32[:, u], cond_hi_sb[:, u].bitcast(F32),
                                        ALU.subtract).then_inc(cond_lo, 1)

            def bias_y(t, u):
                dve.wait_ge(y_mm, t + 1)
                dve.wait_ge(gelus, t + 1)
                nc.vector.tensor_tensor(y32[:, u, :], y_ps[u][:, :], b2_sb[:, :], ALU.add).then_inc(s_then_y, 1)

            def residual(t, u):
                dve.wait_ge(gelus, t + 3)
                row = x1[:, bass.ds(t, 1), :].rearrange("p t l -> p (t l)")
                nc.vector.tensor_tensor(row, row, gelu_sb[:, u, :], ALU.add).then_inc(mix_then_x1, 1)

            def mask_chunk(q):
                dve.wait_ge(s_mm, q + 1)
                if q >= 2:
                    dve.wait_ge(s_hi_ok, q - 1)
                nc.vector.tensor_tensor(s32[:, q % 2, :], s_ps[q][:, :], mask_sb[:, q, :], ALU.mult).then_inc(s_then_y, 1)

            def lo_of_s(q):
                dve.wait_ge(s_hi_ok, q + 1)
                nc.vector.tensor_tensor(s_lo[:, q, :], s32[:, q % 2, :], s_hi[:, q, :].bitcast(F32),
                                        ALU.subtract).then_inc(s_lo_ok, 1)

            dve.wait_ge(mask_in, 16)
            mask_chunk(0)
            dve.wait_ge(bias_mm, 1)
            for v in range(2):
                nc.vector.tensor_copy(mix_bias[:, v * NT // 2:(v + 1) * NT // 2, :],
                                      bias_ps[v][:, :].rearrange("p (t n) -> p t n", n=P)).then_inc(bias_ok, 1)
            lo_of_s(0)
            mask_chunk(1)
            dve.wait_ge(bias_ok, 2)
            bias_cond(0, 0, False)
            lo_of_s(1)
            bias_cond(1, 1, False)
            lo_of_cond(0, 0, False)
            mask_chunk(2)
            lo_of_cond(1, 1, False)
            mask_chunk(3)
            lo_of_s(2)
            lo_of_s(3)
            dve.wait_ge(keys_mm, 1)
            nc.vector.tensor_copy(folded_keys[:, :, :], keys_ps.rearrange("p (q e) -> p q e", q=Q)).then_inc(keys_ok, 1)
            dve.wait_ge(b2_in, 16)
            dve.wait_ge(x1_in, 16)
            dve.wait_ge(mix_ok, 1)
            dve.wait_ge(mix_then_x1, 1)
            bias_y(0, 0)
            with dve.Fori(0, NT // 2 - 1) as q:
                for k, u in ((q * 2 + 1, 1), (q * 2 + 2, 0)):
                    bias_cond(k + 1, 1 - u, True)
                    residual(k - 1, 1 - u)
                    lo_of_cond(k + 1, 1 - u, True)
                    bias_y(k, u)
            residual(NT - 2, 0)

            def z_parts(g, slot_used):
                for u in range(TG):
                    dve.wait_ge(conv_mm, g * TG + u + 1)
                    if slot_used and u == 0:
                        dve.wait_ge(z_hi, g)
                    rows = ctx_rows[:, bass.ds(g * TG + u, 1), :].rearrange("p t (b o) -> p (t b) o", o=C)
                    nc.vector.tensor_tensor(z32[:, :, u * P:(u + 1) * P].rearrange("p q (b o) -> p b q o", o=C),
                                            z_ps[u][:, :].rearrange("p (b q o) -> p b q o", b=BT, o=C),
                                            rows.unsqueeze(2).broadcast_to([P, BT, Q, C]), ALU.add).then_inc(z_ok, 1)
                dve.wait_ge(z_ok, g * TG + TG)
                if slot_used:
                    dve.wait_ge(router_mm, g)
                nc.vector.tensor_reduce(zsum[:, :, :], z32.rearrange("p q (b o) -> p q b o", o=C), AX.X, ALU.add).then_inc(zsum_ok, 1)
                dve.wait_ge(z_hi, g + 1)
                if slot_used:
                    dve.wait_ge(base_mm, g)
                nc.vector.tensor_tensor(z_lo_sb, z32, z_hi_sb.bitcast(F32), ALU.subtract).then_inc(z_lo, 1)

            def router(g):
                dve.wait_ge(router_mm, g + 1)
                nc.vector.tensor_reduce(router_max[:, :], router_ps[0:BG, 0:E], AX.X, ALU.max).then_inc(router_step, 1)
                dve.wait_ge(router_step, g * 3 + 1)
                nc.vector.tensor_scalar(router_bias[:, :], router_max[:, :], -ROUTER_SCALE, None, ALU.mult).then_inc(router_step, 1)
                dve.wait_ge(router_exp_ok, g + 1)
                nc.vector.reciprocal(router_inv[:, :], router_sum[:, :]).then_inc(router_step, 1)
                dve.wait_ge(router_step, g * 3 + 3)
                nc.vector.tensor_scalar(coef[:, :, :], router_exp[:, :].unsqueeze(2).broadcast_to([BG, E, R]), router_inv[:, 0:1], None, ALU.mult).then_inc(coef_ok, 1)
                dve.wait_ge(coef_mm, g + 1)
                nc.vector.tensor_copy(coef_rows[:, :, :], coef_ps.rearrange("p (q b) -> p q b", q=Q)).then_inc(coef_rows_ok, 1)

            def h_parts(g, slot_used):
                dve.wait_ge(coef_rows_ok, g + 1)
                for v in range(2):
                    dve.wait_ge(h_mm, g * 2 + v + 1)
                    if slot_used and v == 0:
                        dve.wait_ge(h_hi, g * 2)
                    nc.vector.tensor_tensor(h32[:, 2 * v:2 * v + 2].rearrange("p q (b o) -> p q b o", o=C),
                                            h_ps[v][:, :].rearrange("p (q b o) -> p q b o", q=2, o=C),
                                            coef_rows[:, 2 * v:2 * v + 2, :].unsqueeze(3).broadcast_to([P, 2, BG, C]),
                                            ALU.mult).then_inc(h_ok, 1)
                for v in range(2):
                    dve.wait_ge(h_hi, g * 2 + v + 1)
                    if slot_used and v == 0:
                        dve.wait_ge(out_mm, g * TG)
                    nc.vector.tensor_tensor(h_lo_sb[:, 2 * v:2 * v + 2], h32[:, 2 * v:2 * v + 2],
                                            h_hi_sb[:, 2 * v:2 * v + 2].bitcast(F32), ALU.subtract).then_inc(h_lo, 1)

            def result(g):
                for u in range(TG):
                    dve.wait_ge(out_mm, g * TG + u + 1)
                    row = x1[:, bass.ds(g * TG + u, 1), :].rearrange("p t l -> p (t l)")
                    nc.vector.tensor_tensor(row, out_ps[u][:, :], row, ALU.add).then_inc(out_ok, 1)

            dve.wait_ge(ctx_ok, 2)
            z_parts(0, False)
            bias_y(NT - 1, 1)
            residual(NT - 1, 1)
            router(0)
            h_parts(0, False)
            with dve.Fori(0, NG - 1) as g:
                z_parts(g + 1, True)
                result(g)
                router(g + 1)
                h_parts(g + 1, True)
            result(NG - 1)

        @block.tensor
        def _(pe):
            def three(dst, lhs_hi, lhs_lo, rhs_hi, rhs_lo, first, last):
                pe.matmul(dst, lhs_hi, rhs_hi, start=first, stop=False)
                pe.matmul(dst, lhs_hi, rhs_lo, start=False, stop=False)
                return pe.matmul(dst, lhs_lo, rhs_hi, start=False, stop=last)

            def s_part(q, d):
                return three(s_ps[q][:, :], w1_hi[:, d, q * P:(q + 1) * P], w1_lo[:, d, q * P:(q + 1) * P],
                             w2_hi[:, d, :], w2_lo[:, d, :], d == 0, d == Q - 1)

            def s_wait(d):
                for s in (w1_hi_ok, w1_lo_ok, w2_hi_ok, w2_lo_ok):
                    pe.wait_ge(s, d + 1)

            def cond(t, u, bank_used):
                pe.wait_ge(x_slot_in[u], t * 8 - u * 8 + 16)
                if bank_used:
                    pe.wait_ge(cond_biased, t - 1)
                rhs = mix[:, bass.ds(t, 1)].rearrange("p t b o -> p (t b o)")
                for q in range(Q):
                    mm = pe.matmul(cond_ps[u][:, q * P:(q + 1) * P], x_slot[:, u, q * P:(q + 1) * P], rhs,
                                   start=True, stop=True)
                mm.then_inc(cond_mm, 1)

            def y(t, u, s_is_new=False):
                pe.wait_ge(cond_hi, t + 1)
                pe.wait_ge(cond_lo, t + 1)
                pe.wait_ge(s_then_y, t + Q - 1)
                for q in range(Q):
                    if s_is_new:
                        pe.wait_ge(s_hi_ok, q + 1)
                        pe.wait_ge(s_lo_ok, q + 1)
                    mm = three(y_ps[u][:, :], cond_hi_sb[:, u, q, :], cond_lo_sb[:, u, q, :], s_hi[:, q, :], s_lo[:, q, :],
                               q == 0, q == Q - 1)
                mm.then_inc(y_mm, 1)

            def context(v):
                return pe.matmul(ctx_ps[v][:, :], ones[:, :],
                                 ctx_rows[:, v * NT // 2:(v + 1) * NT // 2, :].rearrange("p t n -> p (t n)"),
                                 start=True, stop=True)

            def keep_warm(n):
                for _ in range(n):
                    pe.matmul(s_ps[0][:, 0:P], ones[:, :], ones[:, :], start=True, stop=True)

            pe.wait_ge(ones_ok, 1)
            keep_warm(6)
            pe.wait_ge(small_in, 16)
            pe.matmul(h1_ps, part("w0"), part("emb_t"), start=True, stop=True).then_inc(mlp_mm, 1)
            keep_warm(2)
            pe.wait_ge(gelus, 1)
            pe.matmul(h2_ps, part("w1"), h1[:, :], start=True, stop=True).then_inc(mlp_mm, 1)
            pe.wait_ge(ctx_terms, 1)
            context(0)
            pe.wait_ge(gelus, 2)
            pe.matmul(logits_ps, h2[:, :], part("w2"), start=True, stop=True).then_inc(mlp_mm, 1)
            context(1).then_inc(ctx_mm, 1)

            for d in range(2):
                s_wait(d)
                for q in range(Q):
                    s_part(q, d)
                if d == 0:
                    pe.wait_ge(soft, 6)
                    pe.wait_ge(const_in, 16)
                    pe.matmul(att_t_ps, att[:, :], cpart("eye", B), start=True, stop=True)
                    pe.matmul(att_rows_ps, cpart("batch_rows", B), att_tiles[:, :, :].rearrange("b t k -> b (t k)"),
                              start=True, stop=True).then_inc(att_mm, 1)
            for q in range(Q):
                for d in range(2, Q):
                    if q == 0:
                        s_wait(d)
                    mm = s_part(q, d)
                mm.then_inc(s_mm, 1)
                if q == 0:
                    pe.wait_ge(bias_terms, 1)
                    pe.wait_ge(mix_step, 1)
                    for v in range(2):
                        mm = pe.matmul(bias_ps[v][:, :], ones[0:KC, :],
                                       mix_bias[0:KC, v * NT // 2:(v + 1) * NT // 2, :].rearrange("k t n -> k (t n)"),
                                       start=True, stop=True)
                    mm.then_inc(bias_mm, 1)
                if q == 1:
                    pe.wait_ge(mix_ok, 1)
                    pe.wait_ge(ctx_ok, 2)
                    cond(0, 0, False)
                    cond(1, 1, False)
            pe.wait_ge(wq_in, 16)
            pe.wait_ge(bias_ok, 2)
            for q in range(Q):
                mm = pe.matmul(keys_ps[:, q * E:(q + 1) * E], wq_sb[:, q * P:(q + 1) * P], part("keys_t"), start=True, stop=True)
            mm.then_inc(keys_mm, 1)
            y(0, 0, True)
            pe.wait_ge(mix_then_x1, 1)
            with pe.Fori(0, NT // 2 - 1) as p:
                for k, u in ((p * 2 + 1, 1), (p * 2 + 2, 0)):
                    cond(k + 1, 1 - u, True)
                    y(k, u)

            def conv(g, bank_used):
                pe.wait_ge(poly_in, (g + 1) * 16 * BG)
                for u in range(TG):
                    if bank_used:
                        pe.wait_ge(z_ok, g * TG - TG + u + 1)
                    for b in range(BT):
                        for shift in range(3):
                            mm = pe.matmul(z_ps[u][:, b * P:(b + 1) * P], poly[:, u * BT + b, shift:shift + M],
                                           conv_sb[:, shift, :], start=shift == 0, stop=shift == 2)
                    mm.then_inc(conv_mm, 1)

            def router_scores(g):
                pe.wait_ge(zsum_ok, g + 1)
                for q in range(Q):
                    mm = pe.matmul(router_ps[0:BG, 0:E], zsum[:, q, :], folded_keys[:, q, :], start=q == 0, stop=q == Q - 1)
                mm.then_inc(router_mm, 1)

            def h(g, bank_used):
                pe.wait_ge(z_hi, g + 1)
                pe.wait_ge(z_lo, g + 1)
                for c in range(Q):
                    if bank_used and c % 2 == 0:
                        pe.wait_ge(h_ok, g * 2 - 1 + c // 2)
                    for q in range(Q):
                        cols = slice(c * P, (c + 1) * P)
                        mm = three(h_ps[c // 2][:, (c % 2) * NTG:(c % 2 + 1) * NTG], down_hi[:, q, cols], down_lo[:, q, cols],
                                   z_hi_sb[:, q, :], z_lo_sb[:, q, :], q == 0, q == Q - 1)
                    if c % 2:
                        mm.then_inc(h_mm, 1)

            def coef_on_rows(g):
                pe.wait_ge(coef_ok, g + 1)
                for c in range(Q):
                    mm = pe.matmul(coef_ps[:, c * BG:(c + 1) * BG],
                                   coef[:, 2 * c:2 * c + 2, :].rearrange("b e r -> b (e r)"),
                                   cpart("eye", BG)[:, 0:BG], start=True, stop=True)
                mm.then_inc(coef_mm, 1)

            def base(g, bank_used):
                for u in range(TG):
                    if bank_used:
                        pe.wait_ge(out_ok, g * TG - TG + u + 1)
                    for q in range(Q):
                        rows = slice(u * P, (u + 1) * P)
                        mm = three(out_ps[u][:, :], z_hi_sb[:, q, rows], z_lo_sb[:, q, rows], ffn_hi[:, q, :], ffn_lo[:, q, :],
                                   q == 0, False)
                mm.then_inc(base_mm, 1)

            def delta(g):
                pe.wait_ge(h_hi, g * 2 + 2)
                pe.wait_ge(h_lo, g * 2 + 2)
                for u in range(TG):
                    for c in range(Q):
                        rows = slice(u * P, (u + 1) * P)
                        mm = three(out_ps[u][:, :], h_hi_sb[:, c, rows], h_lo_sb[:, c, rows], up_hi[:, c, :], up_lo[:, c, :],
                                   False, c == Q - 1)
                    mm.then_inc(out_mm, 1)

            pe.wait_ge(conv_in, 16)
            conv(0, False)
            y(NT - 1, 1)
            pe.wait_ge(keys_ok, 1)
            router_scores(0)
            pe.wait_ge(down_ok, Q)
            h(0, False)
            coef_on_rows(0)
            pe.wait_ge(ffn_ok, Q)
            pe.wait_ge(s_then_y, Q + NT)
            base(0, False)
            conv(1, True)
            pe.wait_ge(up_ok, Q)
            delta(0)
            with pe.Fori(1, NG - 1) as g:
                router_scores(g)
                h(g, True)
                coef_on_rows(g)
                base(g, True)
                conv(g + 1, True)
                delta(g)
            router_scores(NG - 1)
            h(NG - 1, True)
            coef_on_rows(NG - 1)
            base(NG - 1, True)
            delta(NG - 1)


def kernel(**inputs):
    import numpy as np
    import concourse.bacc as bacc
    from concourse.bass_utils import run_bass_kernel_spmd

    a = {k: np.asarray(v) for k, v in inputs.items()}

    def phases(v):
        return np.ascontiguousarray(np.swapaxes(v.reshape(*v.shape[:-1], M, Q), -1, -2)).reshape(v.shape)

    def chunks(v):
        return np.ascontiguousarray(v.reshape(Q, P, -1).transpose(1, 0, 2))

    def rows_of(v):
        full = np.zeros((P, v.shape[1]), v.dtype)
        full[:v.shape[0]] = v
        return full

    def repeat(v, rows=P):
        return np.repeat(v[None, :], rows, axis=0)

    f = np.float32
    small = {
        "emb_t": a["cond_128"].T, "w0": a["L0_cond_W0"], "b0": a["L0_cond_b0"][:, None], "w1": a["L0_cond_W1"],
        "b1": a["L0_cond_b1"][:, None], "w2": a["L0_cond_W2"], "b2": repeat(a["L0_cond_b2"]),
        "keys_t": a["L0_ffn_lora_keys"].T, "ctx_w_t": a["L0_cond2_c_weight"].T, "ctx_bias": repeat(a["fside_S_0"]),
        "bias_k": rows_of(a["L0_cond_bias_k"]),
    }
    p, b = np.arange(P), np.arange(B)
    const = {
        "eye": rows_of(np.eye(B, dtype=f)),
        "batch_rows": rows_of((b[:, None] % BT == p[None, :] // C).astype(f)),
        "batch_tile": rows_of((b[:, None] // BT == np.arange(NT)[None, :]).astype(f)),
        "own_block": (p[:, None] // C == np.arange(BT)[None, :]).astype(f),
    }
    taps = a["L0_cond2_weight"]
    conv_w = np.zeros((C, Q, 3, Q, C), taps.dtype)
    per = C // GROUPS
    for r in range(Q):
        for s in range(Q):
            for shift in range(3):
                k = Q * (shift - 1) + r - s + PAD
                if 0 <= k < TAPS:
                    for grp in range(GROUPS):
                        own = slice(grp * per, (grp + 1) * per)
                        conv_w[own, r, shift, s, own] = taps[own, :, k].T
    w2t = phases(np.ascontiguousarray(a["L0_attn_w2"].T))
    mask = phases(phases(a["L0_attn_sparse_mask"]).T.copy()).T
    ffn_w = phases(phases(a["L0_ffn_W_org"]).T.copy())
    down = phases(a["L0_ffn_lora_down"].transpose(0, 2, 1)).reshape(E * R, L).T
    arrays = {
        "x": phases(a["x"]).reshape(NT, P, L),
        "small": np.concatenate([small[n] for n, _ in _PACK], axis=1),
        "const": np.concatenate([const[n] for n, _ in _CONST], axis=1),
        "kernels_k": np.tile(a["L0_cond_weight"][..., 0].transpose(2, 1, 0), (BT, 1, 1)),
        "attn_w1": phases(a["L0_attn_w1"]).reshape(Q, P, L),
        "attn_w2t": w2t.reshape(Q, P, L),
        "mask": chunks(mask),
        "attn_b2": repeat(phases(a["L0_attn_b2"])),
        "wq": phases(a["L0_ffn_Wq"]),
        "conv_w": conv_w.reshape(P, 3, P),
        "ffn_w": chunks(ffn_w),
        "lora_down": chunks(down),
        "lora_up": chunks(phases(a["L0_ffn_lora_up"]).reshape(E * R, L)),
    }
    arrays = {f"in_{k}": np.ascontiguousarray(v) for k, v in arrays.items()}
    nc = bacc.Bacc("TRN2", target_bir_lowering=False, num_devices=1)
    args = [nc.dram_tensor(k, v.shape, mybir.dt.from_np(v.dtype), kind="ExternalInput").ap() for k, v in arrays.items()]
    out = nc.dram_tensor("out", (NT, P, L), F32, kind="ExternalOutput").ap()
    adaln_attn_ffn(nc, *args, out)
    r = run_bass_kernel_spmd(nc, [arrays], core_ids=[0])
    got = r.results[0]["out"].reshape(B, C, Q, M)
    return np.ascontiguousarray(got.swapaxes(-1, -2)).reshape(B, C, L)
```

```python
from contextlib import ExitStack

import concourse.bass as bass
from concourse import mybir

ALU = mybir.AluOpType
ACT = mybir.ActivationFunctionType
AX = mybir.AxisListType
F32 = mybir.dt.float32
F32R = mybir.dt.float32r

P = 128
B, C, L = 32, 32, 512
NT = B * C // P
BT = P // C
Q = L // P
KC, TAPS, GROUPS, PAD = 8, 9, 4, 4
E, R = 8, 64
RC = R // Q
HID = 128
PG = C // GROUPS
RP = P // PG
M = L // RP
EDGE = TAPS - 1 - PAD
TG = 2
NG = NT // TG
NH = NT // 2
BG = TG * BT
NTG = TG * P
ROUTER_SCALE = 1.0 / (C * float(P) ** 0.5)

_PACK = [("emb_t", B), ("w0", HID), ("b0", 1), ("w1", HID), ("b1", 1), ("w2", KC), ("b2", KC),
         ("keys_t", E), ("ctx_w_t", C), ("ctx_bias", GROUPS), ("bias_k", C)]
_CONST = [("eye", B), ("batch_rows", P), ("batch_tile", NT), ("own_block", BT)]


def columns(parts):
    at, out = 0, {}
    for name, n in parts:
        out[name] = (at, at + n)
        at += n
    return out, at


PACK, PACK_N = columns(_PACK)
CONST, CONST_N = columns(_CONST)


def adaln_attn_ffn(nc, x, small, const, kernels_k, attn_w1, attn_w2t, mask, attn_b2, wq, conv_w, edge_w,
                   ffn_w, lora_down, lora_up, out):
    with ExitStack() as ctx:
        def sb(name, shape, dt=F32):
            return ctx.enter_context(nc.sbuf_tensor(name, shape, dt))

        def sem(name):
            return ctx.enter_context(nc.semaphore(name))

        small_sb = sb("small_sb", [P, PACK_N])
        const_sb = sb("const_sb", [P, CONST_N])
        ones = sb("ones", [P, P])
        table_dummy = sb("table_dummy", [1, 3])
        kernels_sb = sb("kernels_sb", [P, C, KC])
        wq_sb = sb("wq_sb", [P, L])
        conv_raw = sb("conv_raw", [P, 2, L])
        conv_hi = sb("conv_hi", [P, 2, L], F32R)
        conv_lo = sb("conv_lo", [P, 2, L], F32R)
        b2_sb = sb("b2_sb", [P, L])
        w1_raw = sb("w1_raw", [P, Q, L])
        w2_raw = sb("w2_raw", [P, Q, L])
        w1_hi = sb("w1_hi", [P, Q, L], F32R)
        w1_lo = sb("w1_lo", [P, Q, L], F32R)
        w2_hi = sb("w2_hi", [P, Q, L], F32R)
        w2_lo = sb("w2_lo", [P, Q, L], F32R)
        mask_sb = sb("mask_sb", [P, Q, L])
        s32 = sb("s32", [P, 2, L])
        s_hi = sb("s_hi", [P, Q, L], F32R)
        s_lo = sb("s_lo", [P, Q, L], F32R)
        x_slot = sb("x_slot", [P, 2, L])
        x1 = sb("x1", [P, NT, L])
        cond32 = sb("cond32", [P, 2, Q, P])
        cond_hi_sb = sb("cond_hi_sb", [P, 2, Q, P], F32R)
        cond_lo_sb = sb("cond_lo_sb", [P, 2, Q, P], F32R)
        y_gelu = sb("y_gelu", [P, 4, L])
        y32, gelu_sb = y_gelu[:, 0:2, :], y_gelu[:, 2:4, :]
        down_hi = sb("down_hi", [P, Q, L], F32R)
        down_lo = sb("down_lo", [P, Q, L], F32R)
        ffn_hi = sb("ffn_hi", [P, Q, L], F32R)
        ffn_lo = sb("ffn_lo", [P, Q, L], F32R)
        up_hi = sb("up_hi", [P, Q, L], F32R)
        up_lo = sb("up_lo", [P, Q, L], F32R)
        mix = sb("mix", [P, NT, C, BT])
        mix_rows = sb("mix_rows", [P, NT, C])
        mix_bias = sb("mix_bias", [P, NT, P])
        ctx_w_rep = sb("ctx_w_rep", [P, GROUPS, RP, PG])
        ctx_sb = sb("ctx_sb", [P, GROUPS, B])
        att_rows = sb("att_rows", [P, NT, KC])
        folded_keys = sb("folded_keys", [P, Q, E])
        h1 = sb("h1", [P, B])
        h2 = sb("h2", [P, B])
        logits = sb("logits", [B, KC])
        att_max = sb("att_max", [B, 1])
        att_exp = sb("att_exp", [B, KC])
        att_sum = sb("att_sum", [B, 1])
        att_inv = sb("att_inv", [B, 1])
        att = sb("att", [B, KC])
        att_tiles = sb("att_tiles", [B, NT, KC])
        att_t = sb("att_t", [KC, B])
        zsum = sb("zsum", [P, Q, BG])
        router_max = sb("router_max", [BG, 1])
        router_bias = sb("router_bias", [BG, 1])
        router_exp = sb("router_exp", [BG, E])
        router_sum = sb("router_sum", [BG, 1])
        router_inv = sb("router_inv", [BG, 1])
        coef = sb("coef", [BG, E, RC])
        coef_rows = sb("coef_rows", [P, 2, BG])
        mix_prod = y_gelu[:, :, :].rearrange("p a b -> p (a b)").rearrange("p (t o k) -> p t o k", t=NT, k=KC)
        down_raw, ffn_raw, up_raw = w1_raw, w2_raw, w1_raw
        z32 = mask_sb[:, 0:2, :].rearrange("p a b -> p (a b)").rearrange("p (q n) -> p q n", q=Q)
        h32 = mask_sb[:, 2:4, :].rearrange("p a b -> p (a b)").rearrange("p (q n) -> p q n", q=Q)

        def operand(t):
            return t[:, 0:2, :].rearrange("p a b -> p (a b)").rearrange("p (q n) -> p q n", q=Q)

        z_hi_sb, z_lo_sb, h_hi_sb, h_lo_sb = map(operand, (w1_hi, w1_lo, w2_hi, w2_lo))
        main32, z_nat = s32, cond32[:, :, :, :].rearrange("p a q n -> p (a q n)").rearrange("p (g b m) -> p g b m", g=GROUPS, m=M)
        main_hi, main_lo, edge = w1_hi[:, 2:4, :], w1_lo[:, 2:4, :], w2_hi[:, 2:4, :]
        ER = EDGE * PG

        def edge_view(row, first):
            return edge[row:row + ER].rearrange("p u (c m) -> p (u c) m", m=M)[:, :, first:first + M - 1]

        def main_view(t, row, first):
            return t[row:row + ER].rearrange("p u (c m) -> p (u c) m", m=M)[:, :, first:first + M - 1]

        spilled = nc.dram_tensor("spilled", (NT, RP, P, M), F32, kind="Internal").ap()

        def part(name, rows=P):
            a, b = PACK[name]
            return small_sb[0:rows, a:b]

        def cpart(name, rows=P):
            a, b = CONST[name]
            return const_sb[0:rows, a:b]

        bank = [ctx.enter_context(nc.psum_tensor(f"bank{i}", [P, L], F32)) for i in range(8)]
        s_ps = bank[0:4]
        y_ps, out_ps = bank[0:2], bank[0:2]
        z_ps = bank[2:4]
        cond_ps, h_ps = bank[4:6], bank[4:6]
        ctx_ps = bank[4][:, 0:GROUPS * B]
        bias_ps = bank[6:8]
        mlp_ps = router_ps = bank[6]
        h1_ps, h2_ps, logits_ps = mlp_ps[:, 0:B], mlp_ps[:, B:2 * B], mlp_ps[0:B, 2 * B:2 * B + KC]
        att_t_ps, att_rows_ps = mlp_ps[0:KC, 96:96 + B], mlp_ps[:, 128:128 + NT * KC]
        keys_ps, coef_ps = bank[7][:, 0:Q * E], bank[7][:, 0:BG]

        small_in, const_in, kernels_in, wq_in = sem("small_in"), sem("const_in"), sem("kernels_in"), sem("wq_in")
        conv_in, b2_in, mask_in, x1_in = sem("conv_in"), sem("b2_in"), sem("mask_in"), sem("x1_in")
        conv_w_ok = sem("conv_w_ok")
        w1_in = [sem(f"w1_in{d}") for d in range(Q)]
        w2_in = [sem(f"w2_in{d}") for d in range(Q)]
        down_in, ffn_in, up_in = sem("down_in"), sem("ffn_in"), sem("up_in")
        x_slot_in = [sem(f"x_slot_in{u}") for u in range(2)]
        w1_hi_ok, w1_lo_ok = sem("w1_hi_ok"), sem("w1_lo_ok")
        w2_hi_ok, w2_lo_ok = sem("w2_hi_ok"), sem("w2_lo_ok")
        ones_ok, zeros_ok = sem("ones_ok"), sem("zeros_ok")
        mlp_mm = sem("mlp_mm")
        gelus = sem("gelus")
        soft = sem("soft")
        att_exp_ok, att_mm = sem("att_exp_ok"), sem("att_mm")
        bias_terms, bias_mm, ctx_terms, ctx_mm = sem("bias_terms"), sem("bias_mm"), sem("ctx_terms"), sem("ctx_mm")
        ctx_ok, bias_ok, keys_mm, keys_ok, mix_ok = sem("ctx_ok"), sem("bias_ok"), sem("keys_mm"), sem("keys_ok"), sem("mix_ok")
        mix_step, mix_sums = sem("mix_step"), sem("mix_sums")
        s_mm, s_hi_ok, s_lo_ok = sem("s_mm"), sem("s_hi_ok"), sem("s_lo_ok")
        s_then_y = sem("s_then_y")
        split_hi, down_ok, ffn_ok, up_ok = sem("split_hi"), sem("down_ok"), sem("ffn_ok"), sem("up_ok")
        cond_mm, cond_biased, cond_hi, cond_lo = sem("cond_mm"), sem("cond_biased"), sem("cond_hi"), sem("cond_lo")
        y_mm = sem("y_mm")
        mix_then_x1 = sem("mix_then_x1")
        spill_ok, main_in, prep_hi, prep_lo = sem("spill_ok"), sem("main_in"), sem("prep_hi"), sem("prep_lo")
        conv_mm, z_ok, zt_ok, z_hi, z_lo = sem("conv_mm"), sem("z_ok"), sem("zt_ok"), sem("z_hi"), sem("z_lo")
        zsum_ok, router_mm, router_step, router_exp_ok = sem("zsum_ok"), sem("router_mm"), sem("router_step"), sem("router_exp_ok")
        coef_ok, coef_mm, coef_rows_ok = sem("coef_ok"), sem("coef_mm"), sem("coef_rows_ok")
        h_mm, h_ok, h_hi, h_lo = sem("h_mm"), sem("h_ok"), sem("h_hi"), sem("h_lo")
        base_mm, out_mm, out_ok, out_stored = sem("base_mm"), sem("out_mm"), sem("out_ok"), sem("out_stored")

        block = ctx.enter_context(nc.Block())

        @block.sync
        def _(sp):
            sp.dma_start(small_sb[:, :], small).then_inc(small_in, 16)
            for d in range(Q):
                sp.dma_start(w1_raw[:, d, :], attn_w1[d]).then_inc(w1_in[d], 16)
                sp.dma_start(w2_raw[:, d, :], attn_w2t[d]).then_inc(w2_in[d], 16)
                if d == 1:
                    sp.dma_start(const_sb[:, :], const).then_inc(const_in, 16)
                    sp.dma_start(kernels_sb[:, :, :], kernels_k).then_inc(kernels_in, 16)
            sp.dma_start(mask_sb[:, :, :], mask).then_inc(mask_in, 16)
            for u in range(2):
                sp.dma_start(x_slot[:, u, :], x[u]).then_inc(x_slot_in[u], 16)
            sp.dma_start(b2_sb[:, :], attn_b2).then_inc(b2_in, 16)
            sp.dma_start(wq_sb[:, :], wq).then_inc(wq_in, 16)
            sp.dma_start(x1[:, :, :], x.rearrange("t p l -> p t l")).then_inc(x1_in, 16)
            sp.dma_start(conv_raw[:, 0, :], conv_w).then_inc(conv_in, 16)
            sp.dma_start(conv_raw[:, 1, :], edge_w).then_inc(conv_in, 16)

            def load_slot(t, u):
                sp.wait_ge(cond_mm, t - 1)
                sp.dma_start(x_slot[:, u, :], x[bass.ds(t, 1)].rearrange("t p l -> (t p) l")).then_inc(x_slot_in[u], 16)

            def spill(g):
                sp.wait_ge(mix_then_x1, g * TG + TG + 1)
                for u in range(TG):
                    t = g * TG + u
                    sp.dma_start(spilled[bass.ds(t, 1)].rearrange("t r p m -> p (t r) m"),
                                 x1[:, bass.ds(t, 1), :].rearrange("p t (r m) -> p (t r) m", r=RP)).then_inc(spill_ok, 16)

            def regroup(g):
                sp.wait_ge(spill_ok, g * TG * 16 + TG * 16)
                for u in range(TG):
                    t = g * TG + u
                    sp.dma_start(main32[:, u, :], spilled[bass.ds(t, 1)].rearrange("t r (i c) m -> (t r i) (c m)", i=PG)
                                 ).then_inc(main_in, 16)

            def store(t):
                sp.wait_ge(out_ok, t + 1)
                sp.dma_start(out[bass.ds(t, 1)].rearrange("t p l -> (t p) l"), x1[:, bass.ds(t, 1), :].rearrange("p t l -> p (t l)")).then_inc(out_stored, 16)

            with sp.Fori(1, NT // 2 - 1) as q:
                load_slot(q * 2, 0)
                load_slot(q * 2 + 1, 1)
            spill(0)
            load_slot(NT - 2, 0)
            sp.wait_ge(s_hi_ok, Q)
            sp.wait_ge(s_lo_ok, Q)
            regroup(0)
            load_slot(NT - 1, 1)
            spill(1)
            sp.wait_ge(prep_hi, 3)
            sp.wait_ge(prep_lo, 3)
            regroup(1)
            with sp.Fori(0, NG - 2) as g:
                spill(g + 2)
                sp.wait_ge(prep_hi, g * 3 + 6)
                sp.wait_ge(prep_lo, g * 3 + 6)
                regroup(g + 2)
                store(g * TG)
                store(g * TG + 1)
            for t in range(NT - 2 * TG, NT):
                store(t)
            sp.wait_ge(out_stored, 16 * NT)

        @block.gpsimd
        def _(pool):
            nc.gpsimd.memset(ones[:, :], 1.0).then_inc(ones_ok, 1)
            for d in range(Q):
                pool.wait_ge(w2_hi_ok, d + 1)
                nc.gpsimd.tensor_tensor(w2_lo[:, d, :], w2_raw[:, d, :], w2_hi[:, d, :].bitcast(F32), ALU.subtract).then_inc(w2_lo_ok, 1)

            def split(raw, hi, lo, done, before):
                for d in range(Q):
                    nc.gpsimd.tensor_copy(hi[:, d, :], raw[:, d, :]).then_inc(split_hi, 1)
                    pool.wait_ge(split_hi, before + d + 1)
                    nc.gpsimd.tensor_tensor(lo[:, d, :], raw[:, d, :], hi[:, d, :].bitcast(F32), ALU.subtract).then_inc(done, 1)

            pool.wait_ge(mix_step, 1)
            pool.wait_ge(kernels_in, 16)
            pool.wait_ge(const_in, 16)
            nc.gpsimd.tensor_tensor(mix_prod[:, NH:NT], att_rows[:, NH:NT, :].unsqueeze(2).broadcast_to([P, NH, C, KC]),
                                    kernels_sb[:, :, :].unsqueeze(1).broadcast_to([P, NH, C, KC]),
                                    ALU.mult).then_inc(mix_sums, 1)
            n, left = 1, KC // 2
            while left:
                pool.wait_ge(mix_sums, n)
                sums = mix_prod[:, NH:NT, :, 0:left] if left > 1 else mix_rows[:, NH:NT, :].unsqueeze(3)
                nc.gpsimd.tensor_tensor(sums, mix_prod[:, NH:NT, :, 0:left], mix_prod[:, NH:NT, :, left:2 * left],
                                        ALU.add).then_inc(mix_sums, 1)
                n, left = n + 1, left // 2
            pool.wait_ge(mix_sums, n)
            nc.gpsimd.tensor_tensor(mix[:, NH:NT], mix_rows[:, NH:NT, :].unsqueeze(3).broadcast_to([P, NH, C, BT]),
                                    cpart("own_block").unsqueeze(1).unsqueeze(1).broadcast_to([P, NH, C, BT]),
                                    ALU.mult).then_inc(mix_then_x1, 1)

            pool.wait_ge(w1_hi_ok, Q)
            pool.wait_ge(w1_lo_ok, Q)
            pool.dma_start(down_raw[:, :, :], lora_down).then_inc(down_in, 16)
            pool.wait_ge(conv_in, 32)
            nc.gpsimd.tensor_copy(conv_hi[:, 0, :], conv_raw[:, 0, :]).then_inc(split_hi, 1)
            nc.gpsimd.tensor_copy(conv_hi[:, 1, :], conv_raw[:, 1, :]).then_inc(split_hi, 1)
            pool.wait_ge(split_hi, 2)
            nc.gpsimd.tensor_tensor(conv_lo[:, 0, :], conv_raw[:, 0, :], conv_hi[:, 0, :].bitcast(F32), ALU.subtract).then_inc(conv_w_ok, 1)
            nc.gpsimd.tensor_tensor(conv_lo[0:2 * ER, 1, :], conv_raw[0:2 * ER, 1, :], conv_hi[0:2 * ER, 1, :].bitcast(F32),
                                    ALU.subtract).then_inc(conv_w_ok, 1)
            pool.wait_ge(s_mm, Q)
            nc.gpsimd.memset(edge.bitcast(F32), 0.0).then_inc(zeros_ok, 1)
            pool.wait_ge(down_in, 16)
            pool.wait_ge(w2_hi_ok, Q)
            pool.wait_ge(w2_lo_ok, Q)
            pool.dma_start(ffn_raw[:, :, :], ffn_w).then_inc(ffn_in, 16)
            split(down_raw, down_hi, down_lo, down_ok, 2)
            pool.wait_ge(down_ok, Q)
            pool.dma_start(up_raw[:, :, :], lora_up).then_inc(up_in, 16)
            pool.wait_ge(ffn_in, 16)
            split(ffn_raw, ffn_hi, ffn_lo, ffn_ok, Q + 2)
            pool.wait_ge(up_in, 16)
            split(up_raw, up_hi, up_lo, up_ok, 2 * Q + 2)

        @block.scalar
        def _(act):
            def load_table(func, n):
                nc.scalar.activation(table_dummy[:, n:n + 1], ones[0:1, 0:1], func)

            act.wait_ge(ones_ok, 1)
            load_table(ACT.Gelu, 0)

            def w1_part(d):
                act.wait_ge(w1_in[d], 16)
                nc.scalar.copy(w1_hi[:, d, :], w1_raw[:, d, :]).then_inc(w1_hi_ok, 1)

            act.wait_ge(small_in, 16)
            act.wait_ge(mlp_mm, 1)
            nc.scalar.activation(h1[:, :], h1_ps, ACT.Gelu, bias=part("b0")).then_inc(gelus, 1)
            w1_part(0)
            act.wait_ge(mlp_mm, 2)
            nc.scalar.activation(h2[:, :], h2_ps, ACT.Gelu, bias=part("b1")).then_inc(gelus, 1)
            w1_part(1)
            load_table(ACT.Exp, 1)
            w1_part(2)
            act.wait_ge(soft, 3)
            nc.scalar.activation(att_exp[:, :], logits[:, :], ACT.Exp, accum_out=att_sum[:, :]).then_inc(att_exp_ok, 1)
            w1_part(3)
            load_table(ACT.Gelu, 2)
            def hi_of_s(q):
                act.wait_ge(s_then_y, q + 1)
                nc.scalar.copy(s_hi[:, q, :], s32[:, q % 2, :]).then_inc(s_hi_ok, 1)

            def hi_of_cond(t, u, slot_used):
                act.wait_ge(cond_biased, t + 1)
                if slot_used:
                    act.wait_ge(y_mm, t - 1)
                nc.scalar.copy(cond_hi_sb[:, u], cond32[:, u]).then_inc(cond_hi, 1)

            def gelu(t, u, used):
                act.wait_ge(s_then_y, t + Q + 1)
                act.wait_ge(mix_then_x1, used)
                nc.scalar.activation(gelu_sb[:, u, :], y32[:, u, :], ACT.Gelu).then_inc(gelus, 1)

            hi_of_s(0)
            hi_of_s(1)
            hi_of_cond(0, 0, False)
            hi_of_cond(1, 1, False)
            hi_of_s(2)
            hi_of_s(3)
            gelu(0, 0, 1)
            with act.Fori(0, NT // 2 - 2) as q:
                for k, u in ((q * 2 + 1, 1), (q * 2 + 2, 0)):
                    hi_of_cond(k + 1, 1 - u, True)
                    gelu(k, u, k)

            def prep(g, slot_used):
                act.wait_ge(main_in, g * TG * 16 + TG * 16)
                if slot_used:
                    act.wait_ge(conv_mm, g * 2)
                nc.scalar.copy(main_hi, main32[:, :, :]).then_inc(prep_hi, 1)
                nc.scalar.copy(edge_view(0, 1), main_view(main32, P - ER, 0)).then_inc(prep_hi, 1)
                nc.scalar.copy(edge_view(ER, 0), main_view(main32, 0, 1)).then_inc(prep_hi, 1)

            def hi_of_z(g, slot_used):
                act.wait_ge(zt_ok, g * TG + TG)
                if slot_used:
                    act.wait_ge(base_mm, g)
                nc.scalar.copy(z_hi_sb, z32).then_inc(z_hi, 1)

            def router_exps(g):
                act.wait_ge(router_step, g * 3 + 2)
                nc.scalar.activation(router_exp[:, :], router_ps[0:BG, 0:E], ACT.Exp, bias=router_bias[:, :],
                                     scale=ROUTER_SCALE, accum_out=router_sum[:, :]).then_inc(router_exp_ok, 1)

            def hi_of_h(g, slot_used):
                if slot_used:
                    act.wait_ge(out_mm, g * TG)
                for v in range(2):
                    act.wait_ge(h_ok, g * 2 + v + 1)
                    nc.scalar.copy(h_hi_sb[:, 2 * v:2 * v + 2], h32[:, 2 * v:2 * v + 2]).then_inc(h_hi, 1)

            k = NT - 3
            hi_of_cond(k + 1, 0, True)
            gelu(k, 1, k)
            act.wait_ge(zeros_ok, 1)
            prep(0, False)
            hi_of_cond(k + 2, 1, True)
            gelu(k + 1, 0, k + 1)
            hi_of_z(0, False)
            gelu(NT - 1, 1, NT - 1)
            router_exps(0)
            prep(1, True)
            hi_of_h(0, False)
            with act.Fori(1, NG - 1) as g:
                hi_of_z(g, True)
                router_exps(g)
                prep(g + 1, True)
                hi_of_h(g, True)
            hi_of_z(NG - 1, True)
            router_exps(NG - 1)
            hi_of_h(NG - 1, True)

        @block.vector
        def _(dve):
            def w_parts(d):
                dve.wait_ge(w2_in[d], 16)
                nc.vector.tensor_copy(w2_hi[:, d, :], w2_raw[:, d, :]).then_inc(w2_hi_ok, 1)
                dve.wait_ge(w1_hi_ok, d + 1)
                nc.vector.tensor_tensor(w1_lo[:, d, :], w1_raw[:, d, :], w1_hi[:, d, :].bitcast(F32),
                                        ALU.subtract).then_inc(w1_lo_ok, 1)

            dve.wait_ge(small_in, 16)
            nc.vector.tensor_copy(ctx_w_rep[:, :, :, :],
                                  part("ctx_w_t").rearrange("p (g o) -> p g o", g=GROUPS).unsqueeze(2).broadcast_to([P, GROUPS, RP, PG])
                                  ).then_inc(ctx_terms, 1)
            w_parts(0)
            w_parts(1)
            dve.wait_ge(mlp_mm, 3)
            nc.vector.tensor_tensor(logits[:, :], logits_ps, part("b2", B), ALU.add).then_inc(soft, 1)
            dve.wait_ge(soft, 1)
            nc.vector.tensor_reduce(att_max[:, :], logits[:, :], AX.X, ALU.max).then_inc(soft, 1)
            dve.wait_ge(soft, 2)
            nc.vector.tensor_scalar(logits[:, :], logits[:, :], att_max[:, 0:1], None, ALU.subtract).then_inc(soft, 1)
            dve.wait_ge(ctx_mm, 1)
            nc.vector.tensor_tensor(ctx_sb[:, :, :], ctx_ps.rearrange("p (g b) -> p g b", g=GROUPS),
                                    part("ctx_bias").unsqueeze(2).broadcast_to([P, GROUPS, B]), ALU.add).then_inc(ctx_ok, 1)
            w_parts(2)
            dve.wait_ge(att_exp_ok, 1)
            nc.vector.reciprocal(att_inv[:, :], att_sum[:, :]).then_inc(soft, 1)
            dve.wait_ge(soft, 4)
            nc.vector.tensor_scalar(att[:, :], att_exp[:, :], att_inv[:, 0:1], None, ALU.mult).then_inc(soft, 1)
            dve.wait_ge(soft, 5)
            dve.wait_ge(const_in, 16)
            nc.vector.tensor_tensor(att_tiles[:, :, :], att[:, :].unsqueeze(1).broadcast_to([B, NT, KC]),
                                    cpart("batch_tile", B).unsqueeze(2).broadcast_to([B, NT, KC]),
                                    ALU.mult).then_inc(soft, 1)
            w_parts(3)
            dve.wait_ge(att_mm, 1)
            nc.vector.tensor_copy(att_t[:, :], att_t_ps).then_inc(soft, 1)
            dve.wait_ge(soft, 7)
            nc.vector.tensor_tensor(mix_bias[0:KC].rearrange("k t (o b) -> k t o b", b=BT),
                                    att_t[:, :].rearrange("k (t b) -> k t b", b=BT).unsqueeze(2).broadcast_to([KC, NT, C, BT]),
                                    part("bias_k", KC).unsqueeze(1).unsqueeze(3).broadcast_to([KC, NT, C, BT]),
                                    ALU.mult).then_inc(bias_terms, 1)
            nc.vector.tensor_copy(att_rows[:, :, :], att_rows_ps.rearrange("p (t k) -> p t k", t=NT)).then_inc(mix_step, 1)
            dve.wait_ge(mix_step, 1)
            dve.wait_ge(kernels_in, 16)

            nc.vector.tensor_tensor(mix_prod[:, 0:NH], att_rows[:, 0:NH, :].unsqueeze(2).broadcast_to([P, NH, C, KC]),
                                    kernels_sb[:, :, :].unsqueeze(1).broadcast_to([P, NH, C, KC]),
                                    ALU.mult).then_inc(mix_step, 1)
            dve.wait_ge(mix_step, 2)
            nc.vector.tensor_reduce(mix_rows[:, 0:NH, :], mix_prod[:, 0:NH], AX.X, ALU.add).then_inc(mix_step, 1)
            dve.wait_ge(mix_step, 3)
            nc.vector.tensor_tensor(mix[:, 0:NH], mix_rows[:, 0:NH, :].unsqueeze(3).broadcast_to([P, NH, C, BT]),
                                    cpart("own_block").unsqueeze(1).unsqueeze(1).broadcast_to([P, NH, C, BT]),
                                    ALU.mult).then_inc(mix_ok, 1)

            def bias_cond(t, u, slot_used):
                dve.wait_ge(cond_mm, t + 1)
                if slot_used:
                    dve.wait_ge(cond_hi, t - 1)
                bias = mix_bias[:, bass.ds(t, 1), :].broadcast_to([P, Q, P])
                nc.vector.tensor_tensor(cond32[:, u], cond_ps[u][:, :].rearrange("p (q n) -> p q n", q=Q),
                                        bias, ALU.add).then_inc(cond_biased, 1)

            def lo_of_cond(t, u, slot_used):
                dve.wait_ge(cond_hi, t + 1)
                if slot_used:
                    dve.wait_ge(y_mm, t - 1)
                nc.vector.tensor_tensor(cond_lo_sb[:, u], cond32[:, u], cond_hi_sb[:, u].bitcast(F32),
                                        ALU.subtract).then_inc(cond_lo, 1)

            def bias_y(t, u):
                dve.wait_ge(y_mm, t + 1)
                dve.wait_ge(gelus, t + 1)
                nc.vector.tensor_tensor(y32[:, u, :], y_ps[u][:, :], b2_sb[:, :], ALU.add).then_inc(s_then_y, 1)

            def residual(t, u):
                dve.wait_ge(gelus, t + 3)
                row = x1[:, bass.ds(t, 1), :].rearrange("p t l -> p (t l)")
                nc.vector.tensor_tensor(row, row, gelu_sb[:, u, :], ALU.add).then_inc(mix_then_x1, 1)

            def mask_chunk(q):
                dve.wait_ge(s_mm, q + 1)
                if q >= 2:
                    dve.wait_ge(s_hi_ok, q - 1)
                nc.vector.tensor_tensor(s32[:, q % 2, :], s_ps[q][:, :], mask_sb[:, q, :], ALU.mult).then_inc(s_then_y, 1)

            def lo_of_s(q):
                dve.wait_ge(s_hi_ok, q + 1)
                nc.vector.tensor_tensor(s_lo[:, q, :], s32[:, q % 2, :], s_hi[:, q, :].bitcast(F32),
                                        ALU.subtract).then_inc(s_lo_ok, 1)

            dve.wait_ge(mask_in, 16)
            mask_chunk(0)
            dve.wait_ge(bias_mm, 1)
            for v in range(2):
                nc.vector.tensor_copy(mix_bias[:, v * NT // 2:(v + 1) * NT // 2, :],
                                      bias_ps[v][:, :].rearrange("p (t n) -> p t n", n=P)).then_inc(bias_ok, 1)
            lo_of_s(0)
            mask_chunk(1)
            dve.wait_ge(bias_ok, 2)
            bias_cond(0, 0, False)
            lo_of_s(1)
            bias_cond(1, 1, False)
            lo_of_cond(0, 0, False)
            mask_chunk(2)
            lo_of_cond(1, 1, False)
            mask_chunk(3)
            lo_of_s(2)
            lo_of_s(3)
            dve.wait_ge(keys_mm, 1)
            nc.vector.tensor_copy(folded_keys[:, :, :], keys_ps.rearrange("p (q e) -> p q e", q=Q)).then_inc(keys_ok, 1)
            dve.wait_ge(b2_in, 16)
            dve.wait_ge(x1_in, 16)
            dve.wait_ge(mix_ok, 1)
            dve.wait_ge(mix_then_x1, 1)
            bias_y(0, 0)
            def step(k, u):
                bias_cond(k + 1, 1 - u, True)
                residual(k - 1, 1 - u)
                lo_of_cond(k + 1, 1 - u, True)
                bias_y(k, u)

            def prep(g, slot_used):
                dve.wait_ge(prep_hi, g * 3 + 1)
                if slot_used:
                    dve.wait_ge(conv_mm, g * 2)
                nc.vector.tensor_tensor(main_lo, main32[:, :, :], main_hi.bitcast(F32), ALU.subtract).then_inc(prep_lo, 1)
                dve.wait_ge(prep_lo, g * 3 + 1)
                nc.vector.tensor_copy(edge_view(2 * ER, 1), main_view(main_lo, P - ER, 0).bitcast(F32)).then_inc(prep_lo, 1)
                nc.vector.tensor_copy(edge_view(3 * ER, 0), main_view(main_lo, 0, 1).bitcast(F32)).then_inc(prep_lo, 1)

            with dve.Fori(0, NT // 2 - 2) as q:
                step(q * 2 + 1, 1)
                step(q * 2 + 2, 0)
            step(NT - 3, 1)
            dve.wait_ge(zeros_ok, 1)
            prep(0, False)
            step(NT - 2, 0)
            residual(NT - 2, 0)

            def z_parts(g, slot_used):
                for v in range(2):
                    dve.wait_ge(conv_mm, g * 2 + v + 1)
                    own = slice(2 * v, 2 * v + 2)
                    nc.vector.tensor_tensor(z_nat[:, own], z_ps[v][:, :].rearrange("p (g b m) -> p g b m", g=2, m=M),
                                            ctx_sb[:, own, bass.ds(g * BG, BG)].unsqueeze(3).broadcast_to([P, 2, BG, M]),
                                            ALU.add).then_inc(z_ok, 1)
                dve.wait_ge(z_ok, g * 2 + 2)
                if slot_used:
                    dve.wait_ge(z_hi, g)
                for u in range(TG):
                    nc.vector.transpose(z32[:, :, u * P:(u + 1) * P].rearrange("p q (o c) -> p c q o", o=PG),
                                        z_nat[:, :, u * BT:(u + 1) * BT, :]).then_inc(zt_ok, 1)
                dve.wait_ge(zt_ok, g * TG + TG)
                if slot_used:
                    dve.wait_ge(router_mm, g)
                nc.vector.tensor_reduce(zsum[:, :, :].rearrange("p q (u b) -> p (q u) b", u=TG),
                                        z32.rearrange("p q (u o b) -> p (q u) b o", u=TG, b=BT), AX.X, ALU.add).then_inc(zsum_ok, 1)
                dve.wait_ge(z_hi, g + 1)
                if slot_used:
                    dve.wait_ge(base_mm, g)
                nc.vector.tensor_tensor(z_lo_sb, z32, z_hi_sb.bitcast(F32), ALU.subtract).then_inc(z_lo, 1)

            def router(g):
                dve.wait_ge(router_mm, g + 1)
                nc.vector.tensor_reduce(router_max[:, :], router_ps[0:BG, 0:E], AX.X, ALU.max).then_inc(router_step, 1)
                dve.wait_ge(router_step, g * 3 + 1)
                nc.vector.tensor_scalar(router_bias[:, :], router_max[:, :], -ROUTER_SCALE, None, ALU.mult).then_inc(router_step, 1)
                dve.wait_ge(router_exp_ok, g + 1)
                nc.vector.reciprocal(router_inv[:, :], router_sum[:, :]).then_inc(router_step, 1)
                dve.wait_ge(router_step, g * 3 + 3)
                nc.vector.tensor_scalar(coef[:, :, :], router_exp[:, :].unsqueeze(2).broadcast_to([BG, E, RC]), router_inv[:, 0:1], None, ALU.mult).then_inc(coef_ok, 1)
                dve.wait_ge(coef_mm, g + 1)
                nc.vector.tensor_copy(coef_rows[:, :, :], coef_ps.unsqueeze(1).broadcast_to([P, 2, BG])).then_inc(coef_rows_ok, 1)

            def h_parts(g, slot_used):
                dve.wait_ge(coef_rows_ok, g + 1)
                for v in range(2):
                    dve.wait_ge(h_mm, g * 2 + v + 1)
                    if slot_used and v == 0:
                        dve.wait_ge(h_hi, g * 2)
                    nc.vector.tensor_tensor(h32[:, 2 * v:2 * v + 2].rearrange("p q (u o b) -> p (q u) o b", u=TG, b=BT),
                                            h_ps[v][:, :].rearrange("p (q o b) -> p q o b", o=C, b=BT),
                                            coef_rows[:, :, :].rearrange("p q (u b) -> p (q u) b", u=TG)
                                            .unsqueeze(2).broadcast_to([P, 2 * TG, C, BT]),
                                            ALU.mult).then_inc(h_ok, 1)
                for v in range(2):
                    dve.wait_ge(h_hi, g * 2 + v + 1)
                    if slot_used and v == 0:
                        dve.wait_ge(out_mm, g * TG)
                    nc.vector.tensor_tensor(h_lo_sb[:, 2 * v:2 * v + 2], h32[:, 2 * v:2 * v + 2],
                                            h_hi_sb[:, 2 * v:2 * v + 2].bitcast(F32), ALU.subtract).then_inc(h_lo, 1)

            def result(g):
                for u in range(TG):
                    dve.wait_ge(out_mm, g * TG + u + 1)
                    row = x1[:, bass.ds(g * TG + u, 1), :].rearrange("p t l -> p (t l)")
                    nc.vector.tensor_tensor(row, out_ps[u][:, :], row, ALU.add).then_inc(out_ok, 1)

            dve.wait_ge(ctx_ok, 1)
            z_parts(0, False)
            bias_y(NT - 1, 1)
            residual(NT - 1, 1)
            router(0)
            prep(1, True)
            h_parts(0, False)
            with dve.Fori(1, NG - 1) as g:
                z_parts(g, True)
                result(g - 1)
                router(g)
                prep(g + 1, True)
                h_parts(g, True)
            z_parts(NG - 1, True)
            result(NG - 2)
            router(NG - 1)
            h_parts(NG - 1, True)
            result(NG - 1)

        @block.tensor
        def _(pe):
            def three(dst, lhs_hi, lhs_lo, rhs_hi, rhs_lo, first, last):
                pe.matmul(dst, lhs_hi, rhs_hi, start=first, stop=False)
                pe.matmul(dst, lhs_hi, rhs_lo, start=False, stop=False)
                return pe.matmul(dst, lhs_lo, rhs_hi, start=False, stop=last)

            def s_part(q, d):
                return three(s_ps[q][:, :], w1_hi[:, d, q * P:(q + 1) * P], w1_lo[:, d, q * P:(q + 1) * P],
                             w2_hi[:, d, :], w2_lo[:, d, :], d == 0, d == Q - 1)

            def s_wait(d):
                for s in (w1_hi_ok, w1_lo_ok, w2_hi_ok, w2_lo_ok):
                    pe.wait_ge(s, d + 1)

            def cond(t, u, bank_used):
                pe.wait_ge(x_slot_in[u], t * 8 - u * 8 + 16)
                if bank_used:
                    pe.wait_ge(cond_biased, t - 1)
                rhs = mix[:, bass.ds(t, 1)].rearrange("p t o b -> p (t o b)")
                for q in range(Q):
                    mm = pe.matmul(cond_ps[u][:, q * P:(q + 1) * P], x_slot[:, u, q * P:(q + 1) * P], rhs,
                                   start=True, stop=True)
                mm.then_inc(cond_mm, 1)

            def y(t, u, s_is_new=False):
                pe.wait_ge(cond_hi, t + 1)
                pe.wait_ge(cond_lo, t + 1)
                pe.wait_ge(s_then_y, t + Q - 1)
                for q in range(Q):
                    if s_is_new:
                        pe.wait_ge(s_hi_ok, q + 1)
                        pe.wait_ge(s_lo_ok, q + 1)
                    mm = three(y_ps[u][:, :], cond_hi_sb[:, u, q, :], cond_lo_sb[:, u, q, :], s_hi[:, q, :], s_lo[:, q, :],
                               q == 0, q == Q - 1)
                mm.then_inc(y_mm, 1)

            def keep_warm(n):
                for _ in range(n):
                    pe.matmul(s_ps[0][:, 0:P], ones[:, :], ones[:, :], start=True, stop=True)

            pe.wait_ge(ones_ok, 1)
            keep_warm(6)
            pe.wait_ge(small_in, 16)
            pe.matmul(h1_ps, part("w0"), part("emb_t"), start=True, stop=True).then_inc(mlp_mm, 1)
            keep_warm(2)
            pe.wait_ge(gelus, 1)
            pe.matmul(h2_ps, part("w1"), h1[:, :], start=True, stop=True).then_inc(mlp_mm, 1)
            pe.wait_ge(ctx_terms, 1)
            for g in range(GROUPS):
                mm = pe.matmul(ctx_ps[:, g * B:(g + 1) * B], ctx_w_rep[:, g].rearrange("p r o -> p (r o)"), part("emb_t"),
                               start=True, stop=True)
            mm.then_inc(ctx_mm, 1)
            pe.wait_ge(gelus, 2)
            pe.matmul(logits_ps, h2[:, :], part("w2"), start=True, stop=True).then_inc(mlp_mm, 1)

            for d in range(2):
                s_wait(d)
                for q in range(Q):
                    s_part(q, d)
                if d == 0:
                    pe.wait_ge(soft, 6)
                    pe.wait_ge(const_in, 16)
                    pe.matmul(att_t_ps, att[:, :], cpart("eye", B), start=True, stop=True)
                    pe.matmul(att_rows_ps, cpart("batch_rows", B), att_tiles[:, :, :].rearrange("b t k -> b (t k)"),
                              start=True, stop=True).then_inc(att_mm, 1)
            for q in range(Q):
                for d in range(2, Q):
                    if q == 0:
                        s_wait(d)
                    mm = s_part(q, d)
                mm.then_inc(s_mm, 1)
                if q == 0:
                    pe.wait_ge(bias_terms, 1)
                    pe.wait_ge(mix_step, 1)
                    for v in range(2):
                        mm = pe.matmul(bias_ps[v][:, :], ones[0:KC, :],
                                       mix_bias[0:KC, v * NT // 2:(v + 1) * NT // 2, :].rearrange("k t n -> k (t n)"),
                                       start=True, stop=True)
                    mm.then_inc(bias_mm, 1)
                if q == 1:
                    pe.wait_ge(mix_ok, 1)
                    pe.wait_ge(ctx_ok, 1)
                    cond(0, 0, False)
                    cond(1, 1, False)
            pe.wait_ge(wq_in, 16)
            pe.wait_ge(bias_ok, 2)
            for q in range(Q):
                mm = pe.matmul(keys_ps[:, q * E:(q + 1) * E], wq_sb[:, q * P:(q + 1) * P], part("keys_t"), start=True, stop=True)
            mm.then_inc(keys_mm, 1)
            y(0, 0, True)
            pe.wait_ge(mix_then_x1, 1)
            with pe.Fori(0, NT // 2 - 1) as p:
                for k, u in ((p * 2 + 1, 1), (p * 2 + 2, 0)):
                    cond(k + 1, 1 - u, True)
                    y(k, u)

            def conv(g, bank_used):
                pe.wait_ge(prep_hi, g * 3 + 3)
                pe.wait_ge(prep_lo, g * 3 + 3)
                for v in range(2):
                    if bank_used:
                        pe.wait_ge(z_ok, g * 2 - 1 + v)
                    for grp in (2 * v, 2 * v + 1):
                        cols = slice(grp * P, (grp + 1) * P)
                        dst = z_ps[v][:, (grp % 2) * NTG:(grp % 2 + 1) * NTG].rearrange("p (u n) -> p u n", u=TG)
                        main_w, edge_w_hi, edge_w_lo = conv_hi[:, 0, cols], conv_hi[:, 1, cols], conv_lo[0:2 * ER, 1, cols]
                        pe.matmul(dst, main_w, main_hi[:, :, cols], start=True, stop=False)
                        pe.matmul(dst, main_w, main_lo[:, :, cols], start=False, stop=False)
                        pe.matmul(dst, conv_lo[:, 0, cols], main_hi[:, :, cols], start=False, stop=False)
                        pe.matmul(dst, edge_w_hi, edge[:, :, cols], start=False, stop=False)
                        mm = pe.matmul(dst, edge_w_lo, edge[0:2 * ER, :, cols], start=False, stop=True)
                    mm.then_inc(conv_mm, 1)

            def router_scores(g):
                pe.wait_ge(zsum_ok, g + 1)
                for q in range(Q):
                    mm = pe.matmul(router_ps[0:BG, 0:E], zsum[:, q, :], folded_keys[:, q, :], start=q == 0, stop=q == Q - 1)
                mm.then_inc(router_mm, 1)

            def h(g, bank_used):
                pe.wait_ge(z_hi, g + 1)
                pe.wait_ge(z_lo, g + 1)
                for c in range(Q):
                    if bank_used and c % 2 == 0:
                        pe.wait_ge(h_ok, g * 2 - 1 + c // 2)
                    for q in range(Q):
                        cols = slice(c * P, (c + 1) * P)
                        mm = three(h_ps[c // 2][:, (c % 2) * NTG:(c % 2 + 1) * NTG], down_hi[:, q, cols], down_lo[:, q, cols],
                                   z_hi_sb[:, q, :], z_lo_sb[:, q, :], q == 0, q == Q - 1)
                    if c % 2:
                        mm.then_inc(h_mm, 1)

            def coef_on_rows(g):
                pe.wait_ge(coef_ok, g + 1)
                mm = pe.matmul(coef_ps, coef[:, :, :].rearrange("b e r -> b (e r)"), cpart("eye", BG)[:, 0:BG], start=True, stop=True)
                mm.then_inc(coef_mm, 1)

            def base(g, bank_used):
                for u in range(TG):
                    if bank_used:
                        pe.wait_ge(out_ok, g * TG - TG + u + 1)
                    for q in range(Q):
                        rows = slice(u * P, (u + 1) * P)
                        mm = three(out_ps[u][:, :], z_hi_sb[:, q, rows], z_lo_sb[:, q, rows], ffn_hi[:, q, :], ffn_lo[:, q, :],
                                   q == 0, False)
                mm.then_inc(base_mm, 1)

            def delta(g):
                pe.wait_ge(h_hi, g * 2 + 2)
                pe.wait_ge(h_lo, g * 2 + 2)
                for u in range(TG):
                    for c in range(Q):
                        rows = slice(u * P, (u + 1) * P)
                        mm = three(out_ps[u][:, :], h_hi_sb[:, c, rows], h_lo_sb[:, c, rows], up_hi[:, c, :], up_lo[:, c, :],
                                   False, c == Q - 1)
                    mm.then_inc(out_mm, 1)

            pe.wait_ge(conv_w_ok, 2)
            pe.wait_ge(s_then_y, Q)
            conv(0, False)
            y(NT - 1, 1)
            pe.wait_ge(keys_ok, 1)
            router_scores(0)
            pe.wait_ge(down_ok, Q)
            h(0, False)
            coef_on_rows(0)
            pe.wait_ge(ffn_ok, Q)
            pe.wait_ge(s_then_y, Q + NT)
            base(0, False)
            conv(1, True)
            pe.wait_ge(up_ok, Q)
            delta(0)
            with pe.Fori(1, NG - 1) as g:
                router_scores(g)
                h(g, True)
                coef_on_rows(g)
                base(g, True)
                conv(g + 1, True)
                delta(g)
            router_scores(NG - 1)
            h(NG - 1, True)
            coef_on_rows(NG - 1)
            base(NG - 1, True)
            delta(NG - 1)


def kernel(**inputs):
    import numpy as np
    import concourse.bacc as bacc
    from concourse.bass_utils import run_bass_kernel_spmd

    a = {k: np.asarray(v) for k, v in inputs.items()}

    def phases(v):
        return np.ascontiguousarray(np.swapaxes(v.reshape(*v.shape[:-1], M, RP), -1, -2)).reshape(v.shape)

    def summed(v):
        w = v.reshape(*v.shape[:-1], M, RP // Q, Q)
        return np.ascontiguousarray(np.moveaxis(w, (-1, -2, -3), (-3, -2, -1))).reshape(v.shape)

    def tile_rows(v):
        w = v.reshape(NT, BT, GROUPS, PG, *v.shape[2:])
        return np.ascontiguousarray(np.moveaxis(w, (3, 2, 1), (1, 2, 3))).reshape(NT, P, *v.shape[2:])

    def channels(v, axis):
        w = v.reshape(*v.shape[:axis], GROUPS, PG, *v.shape[axis + 1:])
        return np.ascontiguousarray(np.swapaxes(w, axis, axis + 1)).reshape(v.shape)

    def chunks(v):
        return np.ascontiguousarray(v.reshape(Q, P, -1).transpose(1, 0, 2))

    def rows_of(v):
        full = np.zeros((P, v.shape[1]), v.dtype)
        full[:v.shape[0]] = v
        return full

    def repeat(v, rows=P):
        return np.repeat(v[None, :], rows, axis=0)

    f = np.float32
    small = {
        "emb_t": a["cond_128"].T, "w0": a["L0_cond_W0"], "b0": a["L0_cond_b0"][:, None], "w1": a["L0_cond_W1"],
        "b1": a["L0_cond_b1"][:, None], "w2": a["L0_cond_W2"], "b2": repeat(a["L0_cond_b2"]),
        "keys_t": a["L0_ffn_lora_keys"].T, "ctx_w_t": a["L0_cond2_c_weight"].T, "ctx_bias": np.tile(a["fside_S_0"].reshape(GROUPS, PG).T, (RP, 1)),
        "bias_k": rows_of(channels(a["L0_cond_bias_k"], 1)),
    }
    p, b = np.arange(P), np.arange(B)
    const = {
        "eye": rows_of(np.eye(B, dtype=f)),
        "batch_rows": rows_of((b[:, None] % BT == p[None, :] % BT).astype(f)),
        "batch_tile": rows_of((b[:, None] // BT == np.arange(NT)[None, :]).astype(f)),
        "own_block": (p[:, None] % BT == np.arange(BT)[None, :]).astype(f),
    }
    taps = a["L0_cond2_weight"]
    conv_w = np.zeros((RP, PG, GROUPS, RP, PG), taps.dtype)
    sides = np.zeros((2, EDGE, PG, GROUPS, RP, PG), taps.dtype)
    for grp in range(GROUPS):
        own = taps[grp * PG:(grp + 1) * PG]
        for s in range(RP):
            for k in range(TAPS):
                r = s + k - PAD
                if r < 0:
                    sides[0, r + EDGE, :, grp, s] = own[:, :, k].T
                elif r >= RP:
                    sides[1, r - RP, :, grp, s] = own[:, :, k].T
                else:
                    conv_w[r, :, grp, s] = own[:, :, k].T
    sides = sides.reshape(2 * EDGE * PG, L)
    w2t = phases(np.ascontiguousarray(a["L0_attn_w2"].T))
    mask = phases(phases(a["L0_attn_sparse_mask"]).T.copy()).T
    ffn_w = phases(summed(a["L0_ffn_W_org"]).T.copy())

    def rank_rows(v):
        return np.ascontiguousarray(v.reshape(E, Q, RC, L).transpose(1, 0, 2, 3)).reshape(E * R, L)

    down = rank_rows(summed(a["L0_ffn_lora_down"].transpose(0, 2, 1))).T
    arrays = {
        "x": tile_rows(phases(a["x"])),
        "small": np.concatenate([small[n] for n, _ in _PACK], axis=1),
        "const": np.concatenate([const[n] for n, _ in _CONST], axis=1),
        "kernels_k": np.repeat(channels(channels(a["L0_cond_weight"][..., 0].transpose(2, 1, 0), 0), 1), BT, axis=0),
        "attn_w1": phases(a["L0_attn_w1"]).reshape(Q, P, L),
        "attn_w2t": w2t.reshape(Q, P, L),
        "mask": chunks(mask),
        "attn_b2": repeat(phases(a["L0_attn_b2"])),
        "wq": summed(a["L0_ffn_Wq"]),
        "conv_w": conv_w.reshape(P, L),
        "edge_w": np.concatenate([sides, sides], axis=0),
        "ffn_w": chunks(ffn_w),
        "lora_down": chunks(down),
        "lora_up": chunks(rank_rows(phases(a["L0_ffn_lora_up"]))),
    }
    arrays = {f"in_{k}": np.ascontiguousarray(v) for k, v in arrays.items()}
    nc = bacc.Bacc("TRN2", target_bir_lowering=False, num_devices=1)
    args = [nc.dram_tensor(k, v.shape, mybir.dt.from_np(v.dtype), kind="ExternalInput").ap() for k, v in arrays.items()]
    out = nc.dram_tensor("out", (NT, P, L), F32, kind="ExternalOutput").ap()
    adaln_attn_ffn(nc, *args, out)
    r = run_bass_kernel_spmd(nc, [arrays], core_ids=[0])
    got = r.results[0]["out"].reshape(NT, PG, GROUPS, BT, RP, M).transpose(0, 3, 2, 1, 5, 4)
    return np.ascontiguousarray(got).reshape(B, C, L)
```

```python
from contextlib import ExitStack

import concourse.bass as bass
from concourse import mybir

ALU = mybir.AluOpType
ACT = mybir.ActivationFunctionType
AX = mybir.AxisListType
F32 = mybir.dt.float32
F32R = mybir.dt.float32r

P = 128
B, C, L = 32, 32, 512
NT = B * C // P
BT = P // C
Q = L // P
KC, TAPS, GROUPS, PAD = 8, 9, 4, 4
E, R = 8, 64
RC = R // Q
HID = 128
PG = C // GROUPS
RP = P // PG
M = L // RP
EDGE = TAPS - 1 - PAD
TG = 2
NG = NT // TG
NH = 2
BG = TG * BT
NTG = TG * P
ROUTER_SCALE = 1.0 / (C * float(P) ** 0.5)

_PACK = [("emb_t", B), ("w0", HID), ("b0", 1), ("w1", HID), ("b1", 1), ("w2", KC), ("b2", KC),
         ("keys_t", E), ("ctx_w_t", C), ("ctx_bias", GROUPS)]
_CONST = [("eye", B), ("batch_rows", P), ("batch_tile", NT), ("own_block", BT)]


def columns(parts):
    at, out = 0, {}
    for name, n in parts:
        out[name] = (at, at + n)
        at += n
    return out, at


PACK, PACK_N = columns(_PACK)
CONST, CONST_N = columns(_CONST)


def adaln_attn_ffn(nc, x, small, const, bias_k, kernels_k, attn_w1, attn_w2t, mask, attn_b2, wq, conv_w, edge_w,
                   ffn_w, lora_down, lora_up, out):
    with ExitStack() as ctx:
        def sb(name, shape, dt=F32):
            return ctx.enter_context(nc.sbuf_tensor(name, shape, dt))

        def sem(name):
            return ctx.enter_context(nc.semaphore(name))

        small_sb = sb("small_sb", [P, PACK_N])
        const_sb = sb("const_sb", [P, CONST_N])
        ones = sb("ones", [P, P])
        ones_r = sb("ones_r", [2 * B, P], F32R)
        table_dummy = sb("table_dummy", [1, 3])
        bias_k_sb = sb("bias_k_sb", [B, C, KC])
        kernels_sb = sb("kernels_sb", [P, C, KC])
        wq_sb = sb("wq_sb", [P, L])
        conv_raw = sb("conv_raw", [P, 2, L])
        conv_hi = sb("conv_hi", [P, 2, L], F32R)
        conv_lo = sb("conv_lo", [P, 2, L], F32R)
        b2_sb = sb("b2_sb", [P, L])
        w1_raw = sb("w1_raw", [P, Q, L])
        w2_raw = sb("w2_raw", [P, Q, L])
        w1_hi = sb("w1_hi", [P, Q, L], F32R)
        w1_lo = sb("w1_lo", [P, Q, L], F32R)
        w2_hi = sb("w2_hi", [P, Q, L], F32R)
        w2_lo = sb("w2_lo", [P, Q, L], F32R)
        mask_sb = sb("mask_sb", [P, Q, L])
        s32 = sb("s32", [P, 2, L])
        s_hi = sb("s_hi", [P, Q, L], F32R)
        s_lo = sb("s_lo", [P, Q, L], F32R)
        x_slot = sb("x_slot", [P, 2, L])
        x1 = sb("x1", [P, NT, L])
        cond32 = sb("cond32", [P, 2, Q, P])
        cond_hi_sb = sb("cond_hi_sb", [P, 2, Q, P], F32R)
        cond_lo_sb = sb("cond_lo_sb", [P, 2, Q, P], F32R)
        y_gelu = sb("y_gelu", [P, 4, L])
        y32, gelu_sb = y_gelu[:, 0:2, :], y_gelu[:, 2:4, :]
        down_hi = sb("down_hi", [P, Q, L], F32R)
        down_lo = sb("down_lo", [P, Q, L], F32R)
        ffn_hi = sb("ffn_hi", [P, Q, L], F32R)
        ffn_lo = sb("ffn_lo", [P, Q, L], F32R)
        up_hi = sb("up_hi", [P, Q, L], F32R)
        up_lo = sb("up_lo", [P, Q, L], F32R)
        mix = sb("mix", [P, NT, C, BT])
        mix_rows = sb("mix_rows", [P, NT, C])
        mix_bias = sb("mix_bias", [P, NT, P])
        ctx_w_rep = sb("ctx_w_rep", [P, GROUPS, RP, PG])
        ctx_sb = sb("ctx_sb", [P, GROUPS, B])
        att_rows = sb("att_rows", [P, NT, KC])
        folded_keys = sb("folded_keys", [P, Q, E])
        h1 = sb("h1", [P, B])
        h2 = sb("h2", [P, B])
        logits = sb("logits", [B, KC])
        att_max = sb("att_max", [B, 1])
        att_exp = sb("att_exp", [B, KC])
        att_sum = sb("att_sum", [B, 1])
        att_inv = sb("att_inv", [B, 1])
        att = sb("att", [B, KC])
        att_tiles = sb("att_tiles", [B, NT, KC])
        agg = sb("agg", [B, C])
        agg_terms = sb("agg_terms", [B, C, KC])
        agg_parts = sb("agg_parts", [2 * B, C], F32R)
        zsum = sb("zsum", [P, Q, BG])
        router_max = sb("router_max", [BG, 1])
        router_bias = sb("router_bias", [BG, 1])
        router_exp = sb("router_exp", [BG, E])
        router_sum = sb("router_sum", [BG, 1])
        router_inv = sb("router_inv", [BG, 1])
        coef = sb("coef", [BG, E, RC])
        coef_rows = sb("coef_rows", [P, 2, BG])
        mix_prod = y_gelu[:, :, :].rearrange("p a b -> p (a b)").rearrange("p (t o k) -> p t o k", t=NT, k=KC)
        bias_terms_sb = down_hi[0:2 * B, 0:2, :].rearrange("p a b -> p (a b)").rearrange("p (t n) -> p t n", t=NT)
        down_raw, ffn_raw, up_raw = w1_raw, w2_raw, w1_raw
        z32 = mask_sb[:, 0:2, :].rearrange("p a b -> p (a b)").rearrange("p (q n) -> p q n", q=Q)
        h32 = mask_sb[:, 2:4, :].rearrange("p a b -> p (a b)").rearrange("p (q n) -> p q n", q=Q)

        def operand(t):
            return t[:, 0:2, :].rearrange("p a b -> p (a b)").rearrange("p (q n) -> p q n", q=Q)

        z_hi_sb, z_lo_sb, h_hi_sb, h_lo_sb = map(operand, (w1_hi, w1_lo, w2_hi, w2_lo))
        main32, z_nat = s32, cond32[:, :, :, :].rearrange("p a q n -> p (a q n)").rearrange("p (g b m) -> p g b m", g=GROUPS, m=M)
        main_hi, main_lo, edge = w1_hi[:, 2:4, :], w1_lo[:, 2:4, :], w2_hi[:, 2:4, :]
        ER = EDGE * PG

        def edge_view(row, first):
            return edge[row:row + ER].rearrange("p u (c m) -> p (u c) m", m=M)[:, :, first:first + M - 1]

        def main_view(t, row, first):
            return t[row:row + ER].rearrange("p u (c m) -> p (u c) m", m=M)[:, :, first:first + M - 1]

        spilled = nc.dram_tensor("spilled", (NT, RP, P, M), F32, kind="Internal").ap()

        def half(v):
            return slice(v * L // 2, (v + 1) * L // 2)

        def part(name, rows=P):
            a, b = PACK[name]
            return small_sb[0:rows, a:b]

        def cpart(name, rows=P):
            a, b = CONST[name]
            return const_sb[0:rows, a:b]

        bank = [ctx.enter_context(nc.psum_tensor(f"bank{i}", [P, L], F32)) for i in range(8)]
        s_ps = bank[0:4]
        y_ps, out_ps = bank[0:2], bank[0:2]
        z_ps = bank[2:4]
        last_ps = (bank[1], bank[2])
        cond_ps, h_ps = bank[4:6], bank[4:6]
        ctx_ps = bank[4][:, 0:GROUPS * B]
        bias_ps = bank[6:8]
        mlp_ps = router_ps = bank[6]
        h1_ps, h2_ps, logits_ps = mlp_ps[:, 0:B], mlp_ps[:, B:2 * B], mlp_ps[0:B, 2 * B:2 * B + KC]
        att_rows_ps = mlp_ps[:, 128:128 + NT * KC]
        keys_ps, coef_ps = bank[7][:, 0:Q * E], bank[7][:, 0:BG]

        small_in, const_in, kernels_in, wq_in = sem("small_in"), sem("const_in"), sem("kernels_in"), sem("wq_in")
        x1_late_in = sem("x1_late_in")
        conv_in, b2_in, mask_in, x1_in = sem("conv_in"), sem("b2_in"), sem("mask_in"), sem("x1_in")
        conv_w_ok = sem("conv_w_ok")
        w1_in = [sem(f"w1_in{d}") for d in range(Q)]
        w2_in = [sem(f"w2_in{d}") for d in range(Q)]
        down_in, ffn_in, up_in = sem("down_in"), sem("ffn_in"), sem("up_in")
        x_slot_in = [sem(f"x_slot_in{u}") for u in range(2)]
        w1_hi_ok, w1_lo_ok = sem("w1_hi_ok"), sem("w1_lo_ok")
        w2_hi_ok, w2_lo_ok = sem("w2_hi_ok"), sem("w2_lo_ok")
        ones_ok, zeros_ok, ones_r_ok = sem("ones_ok"), sem("zeros_ok"), sem("ones_r_ok")
        mlp_mm = sem("mlp_mm")
        gelus = sem("gelus")
        bias_k_in, agg_step, agg_ok = sem("bias_k_in"), sem("agg_step"), sem("agg_ok")
        soft = sem("soft")
        att_exp_ok, att_mm = sem("att_exp_ok"), sem("att_mm")
        bias_terms, bias_mm, ctx_terms, ctx_mm = sem("bias_terms"), sem("bias_mm"), sem("ctx_terms"), sem("ctx_mm")
        ctx_ok, bias_ok, keys_mm, keys_ok, mix_ok = sem("ctx_ok"), sem("bias_ok"), sem("keys_mm"), sem("keys_ok"), sem("mix_ok")
        mix_step, mix_sums = sem("mix_step"), sem("mix_sums")
        s_mm, s_hi_ok, s_lo_ok = sem("s_mm"), sem("s_hi_ok"), sem("s_lo_ok")
        s_then_y = sem("s_then_y")
        down_hi_ok, ffn_hi_ok, up_hi_ok = sem("down_hi_ok"), sem("ffn_hi_ok"), sem("up_hi_ok")
        split_hi, down_ok, ffn_ok, up_ok = sem("split_hi"), sem("down_ok"), sem("ffn_ok"), sem("up_ok")
        cond_mm, cond_biased, cond_hi, cond_lo = sem("cond_mm"), sem("cond_biased"), sem("cond_hi"), sem("cond_lo")
        y_mm = sem("y_mm")
        mix_then_x1 = sem("mix_then_x1")
        spill_ok, main_in, prep_hi, prep_lo = sem("spill_ok"), sem("main_in"), sem("prep_hi"), sem("prep_lo")
        conv_mm, z_ok, zt_ok, z_hi, z_lo = sem("conv_mm"), sem("z_ok"), sem("zt_ok"), sem("z_hi"), sem("z_lo")
        zsum_ok, router_mm, router_step, router_exp_ok = sem("zsum_ok"), sem("router_mm"), sem("router_step"), sem("router_exp_ok")
        coef_ok, coef_mm, coef_rows_ok = sem("coef_ok"), sem("coef_mm"), sem("coef_rows_ok")
        h_mm, h_ok, h_hi, h_lo = sem("h_mm"), sem("h_ok"), sem("h_hi"), sem("h_lo")
        base_mm, out_mm, out_ok, out_stored = sem("base_mm"), sem("out_mm"), sem("out_ok"), sem("out_stored")

        block = ctx.enter_context(nc.Block())

        @block.sync
        def _(sp):
            sp.dma_start(small_sb[:, :], small).then_inc(small_in, 16)
            for d in range(Q):
                sp.dma_start(w1_raw[:, d, :], attn_w1[d]).then_inc(w1_in[d], 16)
                sp.dma_start(w2_raw[:, d, :], attn_w2t[d]).then_inc(w2_in[d], 16)
                if d == 1:
                    sp.dma_start(const_sb[:, :], const).then_inc(const_in, 16)
                    sp.dma_start(bias_k_sb[:, :, :], bias_k).then_inc(bias_k_in, 16)
                    sp.dma_start(kernels_sb[:, :, :], kernels_k).then_inc(kernels_in, 16)
            sp.dma_start(mask_sb[:, :, :], mask).then_inc(mask_in, 16)
            for u in range(2):
                sp.dma_start(x_slot[:, u, :], x[u]).then_inc(x_slot_in[u], 16)
            sp.dma_start(b2_sb[:, :], attn_b2).then_inc(b2_in, 16)
            sp.dma_start(wq_sb[:, :], wq).then_inc(wq_in, 16)

            def load_slot(t, u):
                sp.wait_ge(cond_mm, t - 1)
                sp.dma_start(x_slot[:, u, :], x[bass.ds(t, 1)].rearrange("t p l -> (t p) l")).then_inc(x_slot_in[u], 16)

            def spill(t):
                sp.wait_ge(mix_then_x1, t + 2)
                sp.dma_start(spilled[bass.ds(t, 1)].rearrange("t r p m -> p (t r) m"),
                             x1[:, bass.ds(t, 1), :].rearrange("p t (r m) -> p (t r) m", r=RP)).then_inc(spill_ok, 16)

            def regroup(g):
                sp.wait_ge(spill_ok, g * TG * 16 + TG * 16)
                for u in range(TG):
                    t = g * TG + u
                    sp.dma_start(main32[:, u, :], spilled[bass.ds(t, 1)].rearrange("t r (i c) m -> (t r i) (c m)", i=PG)
                                 ).then_inc(main_in, 16)

            def store(t):
                sp.wait_ge(out_ok, t + 1)
                sp.dma_start(out[bass.ds(t, 1)].rearrange("t p l -> (t p) l"), x1[:, bass.ds(t, 1), :].rearrange("p t l -> p (t l)")).then_inc(out_stored, 16)

            def load_x1(first, there):
                tiles = slice(first, first + NT // 2)
                sp.dma_start(x1[:, tiles, :], x[tiles].rearrange("t p l -> p t l")).then_inc(there, 16)

            load_x1(0, x1_in)
            for s in (w1_hi_ok, w1_lo_ok, w2_hi_ok, w2_lo_ok):
                sp.wait_ge(s, Q)
            sp.dma_start(down_raw[:, :, :], lora_down).then_inc(down_in, 16)
            load_slot(2, 0)
            load_slot(3, 1)
            sp.dma_start(conv_raw[:, 0, :], conv_w).then_inc(conv_in, 16)
            sp.dma_start(conv_raw[:, 1, :], edge_w).then_inc(conv_in, 16)
            load_x1(NT // 2, x1_late_in)
            for t in range(TG):
                load_slot(t + 4, t % 2)
                spill(t)
            load_slot(NT - 2, 0)
            sp.wait_ge(s_hi_ok, Q)
            sp.wait_ge(s_lo_ok, Q)
            regroup(0)
            load_slot(NT - 1, 1)
            sp.dma_start(ffn_raw[:, :, :], ffn_w).then_inc(ffn_in, 16)
            spill(2)
            spill(3)
            sp.wait_ge(prep_hi, 3)
            sp.wait_ge(prep_lo, 3)
            regroup(1)
            with sp.Fori(0, NG - 2) as g:
                spill(g * TG + 2 * TG)
                spill(g * TG + 2 * TG + 1)
                sp.wait_ge(prep_hi, g * 3 + 6)
                sp.wait_ge(prep_lo, g * 3 + 6)
                regroup(g + 2)
                store(g * TG)
                store(g * TG + 1)
            for t in range(NT - 2 * TG, NT - 1):
                store(t)
            for v in range(2):
                sp.wait_ge(out_ok, NT + v)
                sp.dma_start(out[NT - 1, :, half(v)], x1[:, NT - 1, half(v)]).then_inc(out_stored, 16)
            sp.wait_ge(out_stored, 16 * (NT + 1))

        @block.gpsimd
        def _(pool):
            nc.gpsimd.memset(ones[:, :], 1.0).then_inc(ones_ok, 1)
            nc.gpsimd.memset(ones_r[:, :].bitcast(F32), 1.0).then_inc(ones_r_ok, 1)
            for d in range(Q):
                pool.wait_ge(w2_hi_ok, d + 1)
                nc.gpsimd.tensor_tensor(w2_lo[:, d, :], w2_raw[:, d, :], w2_hi[:, d, :].bitcast(F32), ALU.subtract).then_inc(w2_lo_ok, 1)

            def lo_parts(raw, hi, lo, hi_ok, done):
                for d in range(Q):
                    pool.wait_ge(hi_ok, d + 1)
                    nc.gpsimd.tensor_tensor(lo[:, d, :], raw[:, d, :], hi[:, d, :].bitcast(F32), ALU.subtract).then_inc(done, 1)

            pool.wait_ge(agg_ok, 2)
            pool.wait_ge(const_in, 16)
            nc.gpsimd.tensor_tensor(bias_terms_sb.rearrange("k t (o b) -> k t o b", b=BT),
                                    agg_parts[:, :].bitcast(F32).unsqueeze(1).unsqueeze(3).broadcast_to([2 * B, NT, C, BT]),
                                    cpart("eye", 2 * B).rearrange("k (t b) -> k t b", b=BT).unsqueeze(2).broadcast_to([2 * B, NT, C, BT]),
                                    ALU.mult).then_inc(bias_terms, 1)
            pool.wait_ge(mix_step, 1)
            pool.wait_ge(kernels_in, 16)
            pool.wait_ge(const_in, 16)
            nc.gpsimd.tensor_tensor(mix_prod[:, NH:NT], att_rows[:, NH:NT, :].unsqueeze(2).broadcast_to([P, NT - NH, C, KC]),
                                    kernels_sb[:, :, :].unsqueeze(1).broadcast_to([P, NT - NH, C, KC]),
                                    ALU.mult).then_inc(mix_sums, 1)
            n, left = 1, KC // 2
            while left:
                pool.wait_ge(mix_sums, n)
                sums = mix_prod[:, NH:NT, :, 0:left] if left > 1 else mix_rows[:, NH:NT, :].unsqueeze(3)
                nc.gpsimd.tensor_tensor(sums, mix_prod[:, NH:NT, :, 0:left], mix_prod[:, NH:NT, :, left:2 * left],
                                        ALU.add).then_inc(mix_sums, 1)
                n, left = n + 1, left // 2
            pool.wait_ge(mix_sums, n)
            nc.gpsimd.tensor_tensor(mix[:, NH:NT], mix_rows[:, NH:NT, :].unsqueeze(3).broadcast_to([P, NT - NH, C, BT]),
                                    cpart("own_block").unsqueeze(1).unsqueeze(1).broadcast_to([P, NT - NH, C, BT]),
                                    ALU.mult).then_inc(mix_then_x1, 1)

            pool.wait_ge(conv_in, 32)
            nc.gpsimd.tensor_copy(conv_hi[:, 0, :], conv_raw[:, 0, :]).then_inc(split_hi, 1)
            nc.gpsimd.tensor_copy(conv_hi[:, 1, :], conv_raw[:, 1, :]).then_inc(split_hi, 1)
            pool.wait_ge(split_hi, 2)
            nc.gpsimd.tensor_tensor(conv_lo[:, 0, :], conv_raw[:, 0, :], conv_hi[:, 0, :].bitcast(F32), ALU.subtract).then_inc(conv_w_ok, 1)
            nc.gpsimd.tensor_tensor(conv_lo[0:2 * ER, 1, :], conv_raw[0:2 * ER, 1, :], conv_hi[0:2 * ER, 1, :].bitcast(F32),
                                    ALU.subtract).then_inc(conv_w_ok, 1)
            pool.wait_ge(s_mm, Q)
            nc.gpsimd.memset(edge.bitcast(F32), 0.0).then_inc(zeros_ok, 1)
            lo_parts(down_raw, down_hi, down_lo, down_hi_ok, down_ok)
            pool.wait_ge(down_ok, Q)
            pool.dma_start(up_raw[:, :, :], lora_up).then_inc(up_in, 16)
            lo_parts(ffn_raw, ffn_hi, ffn_lo, ffn_hi_ok, ffn_ok)
            lo_parts(up_raw, up_hi, up_lo, up_hi_ok, up_ok)

        @block.scalar
        def _(act):
            def load_table(func, n):
                nc.scalar.activation(table_dummy[:, n:n + 1], ones[0:1, 0:1], func)

            act.wait_ge(ones_ok, 1)
            load_table(ACT.Gelu, 0)

            def w1_part(d):
                act.wait_ge(w1_in[d], 16)
                nc.scalar.copy(w1_hi[:, d, :], w1_raw[:, d, :]).then_inc(w1_hi_ok, 1)

            w1_part(0)
            act.wait_ge(small_in, 16)
            act.wait_ge(mlp_mm, 1)
            nc.scalar.activation(h1[:, :], h1_ps, ACT.Gelu, bias=part("b0")).then_inc(gelus, 1)
            act.wait_ge(mlp_mm, 2)
            nc.scalar.activation(h2[:, :], h2_ps, ACT.Gelu, bias=part("b1")).then_inc(gelus, 1)
            w1_part(1)
            load_table(ACT.Exp, 1)
            w1_part(2)
            act.wait_ge(soft, 3)
            nc.scalar.activation(att_exp[:, :], logits[:, :], ACT.Exp, accum_out=att_sum[:, :]).then_inc(att_exp_ok, 1)
            w1_part(3)
            load_table(ACT.Gelu, 2)
            def hi_of_s(q):
                act.wait_ge(s_then_y, q + 1)
                nc.scalar.copy(s_hi[:, q, :], s32[:, q % 2, :]).then_inc(s_hi_ok, 1)

            def hi_of_cond(t, u, slot_used):
                act.wait_ge(cond_biased, t + 1)
                if slot_used:
                    act.wait_ge(y_mm, t - 1)
                nc.scalar.copy(cond_hi_sb[:, u], cond32[:, u]).then_inc(cond_hi, 1)

            def gelu(t, u, used):
                act.wait_ge(s_then_y, t + Q + 1)
                act.wait_ge(mix_then_x1, used)
                nc.scalar.activation(gelu_sb[:, u, :], y32[:, u, :], ACT.Gelu).then_inc(gelus, 1)

            hi_of_s(0)
            act.wait_ge(bias_mm, 1)
            for v in range(2):
                nc.scalar.copy(mix_bias[:, v * NT // 2:(v + 1) * NT // 2, :],
                                      bias_ps[v][:, :].rearrange("p (t n) -> p t n", n=P)).then_inc(bias_ok, 1)
            hi_of_s(1)
            hi_of_cond(0, 0, False)
            hi_of_s(2)
            hi_of_cond(1, 1, False)
            hi_of_s(3)
            gelu(0, 0, 1)
            with act.Fori(0, NT // 2 - 2) as q:
                for k, u in ((q * 2 + 1, 1), (q * 2 + 2, 0)):
                    hi_of_cond(k + 1, 1 - u, True)
                    act.wait_ge(down_in, 16)
                    nc.scalar.copy(down_hi[:, bass.ds(k - 1, 1), :], down_raw[:, bass.ds(k - 1, 1), :]).then_inc(down_hi_ok, 1)
                    gelu(k, u, k)

            def main_hi_part(g, slot_used):
                act.wait_ge(main_in, g * TG * 16 + TG * 16)
                if slot_used:
                    act.wait_ge(conv_mm, g * 2)
                nc.scalar.copy(main_hi, main32[:, :, :]).then_inc(prep_hi, 1)

            def edge_hi_parts():
                nc.scalar.copy(edge_view(0, 1), main_view(main32, P - ER, 0)).then_inc(prep_hi, 1)
                nc.scalar.copy(edge_view(ER, 0), main_view(main32, 0, 1)).then_inc(prep_hi, 1)

            def hi_of_z(g, slot_used):
                act.wait_ge(zt_ok, g * TG + TG)
                if slot_used:
                    act.wait_ge(base_mm, g)
                for v in range(2):
                    own = slice(2 * v, 2 * v + 2)
                    nc.scalar.copy(z_hi_sb[:, own, :], z32[:, own, :]).then_inc(z_hi, 1)

            def router_exps(g):
                act.wait_ge(router_step, g * 3 + 2)
                nc.scalar.activation(router_exp[:, :], router_ps[0:BG, 0:E], ACT.Exp, bias=router_bias[:, :],
                                     scale=ROUTER_SCALE, accum_out=router_sum[:, :]).then_inc(router_exp_ok, 1)

            def hi_of_h(g, slot_used):
                if slot_used:
                    act.wait_ge(out_mm, g * TG)
                for v in range(2):
                    act.wait_ge(h_ok, g * 2 + v + 1)
                    nc.scalar.copy(h_hi_sb[:, 2 * v:2 * v + 2], h32[:, 2 * v:2 * v + 2]).then_inc(h_hi, 1)

            def hi_parts(raw, hi, there, done, chunks=range(Q)):
                act.wait_ge(there, 16)
                for d in chunks:
                    nc.scalar.copy(hi[:, d, :], raw[:, d, :]).then_inc(done, 1)

            k = NT - 3
            main_hi_part(0, False)
            hi_of_cond(k + 1, 0, True)
            act.wait_ge(zeros_ok, 1)
            edge_hi_parts()
            gelu(k, 1, k)
            hi_of_cond(k + 2, 1, True)
            hi_parts(ffn_raw, ffn_hi, ffn_in, ffn_hi_ok)
            hi_of_z(0, False)
            gelu(k + 1, 0, k + 1)
            hi_parts(up_raw, up_hi, up_in, up_hi_ok, (0, 1))
            gelu(NT - 1, 1, NT - 1)
            router_exps(0)
            main_hi_part(1, True)
            edge_hi_parts()
            hi_parts(up_raw, up_hi, up_in, up_hi_ok, (2, 3))
            hi_of_h(0, False)
            with act.Fori(1, NG - 1) as g:
                hi_of_z(g, True)
                router_exps(g)
                main_hi_part(g + 1, True)
                edge_hi_parts()
                hi_of_h(g, True)
            hi_of_z(NG - 1, True)
            router_exps(NG - 1)
            hi_of_h(NG - 1, True)

        @block.vector
        def _(dve):
            def w_parts(d):
                dve.wait_ge(w2_in[d], 16)
                nc.vector.tensor_copy(w2_hi[:, d, :], w2_raw[:, d, :]).then_inc(w2_hi_ok, 1)
                dve.wait_ge(w1_hi_ok, d + 1)
                nc.vector.tensor_tensor(w1_lo[:, d, :], w1_raw[:, d, :], w1_hi[:, d, :].bitcast(F32),
                                        ALU.subtract).then_inc(w1_lo_ok, 1)

            dve.wait_ge(small_in, 16)
            nc.vector.tensor_copy(ctx_w_rep[:, :, :, :],
                                  part("ctx_w_t").rearrange("p (g o) -> p g o", g=GROUPS).unsqueeze(2).broadcast_to([P, GROUPS, RP, PG])
                                  ).then_inc(ctx_terms, 1)
            w_parts(0)
            w_parts(1)
            dve.wait_ge(mlp_mm, 3)
            nc.vector.tensor_tensor(logits[:, :], logits_ps, part("b2", B), ALU.add).then_inc(soft, 1)
            dve.wait_ge(soft, 1)
            nc.vector.tensor_reduce(att_max[:, :], logits[:, :], AX.X, ALU.max).then_inc(soft, 1)
            dve.wait_ge(soft, 2)
            nc.vector.tensor_scalar(logits[:, :], logits[:, :], att_max[:, 0:1], None, ALU.subtract).then_inc(soft, 1)
            w_parts(2)
            dve.wait_ge(att_exp_ok, 1)
            nc.vector.reciprocal(att_inv[:, :], att_sum[:, :]).then_inc(soft, 1)
            dve.wait_ge(soft, 4)
            nc.vector.tensor_scalar(att[:, :], att_exp[:, :], att_inv[:, 0:1], None, ALU.mult).then_inc(soft, 1)
            dve.wait_ge(soft, 5)
            dve.wait_ge(const_in, 16)
            nc.vector.tensor_tensor(att_tiles[:, :, :], att[:, :].unsqueeze(1).broadcast_to([B, NT, KC]),
                                    cpart("batch_tile", B).unsqueeze(2).broadcast_to([B, NT, KC]),
                                    ALU.mult).then_inc(soft, 1)
            w_parts(3)
            dve.wait_ge(ctx_mm, 1)
            nc.vector.tensor_tensor(ctx_sb[:, :, :], ctx_ps.rearrange("p (g b) -> p g b", g=GROUPS),
                                    part("ctx_bias").unsqueeze(2).broadcast_to([P, GROUPS, B]), ALU.add).then_inc(ctx_ok, 1)
            dve.wait_ge(bias_k_in, 16)
            dve.wait_ge(soft, 5)
            nc.vector.tensor_tensor(agg_terms[:, :, :], att[:, :].unsqueeze(1).broadcast_to([B, C, KC]), bias_k_sb[:, :, :],
                                    ALU.mult).then_inc(agg_step, 1)
            dve.wait_ge(agg_step, 1)
            nc.vector.tensor_reduce(agg[:, :], agg_terms[:, :, :], AX.X, ALU.add).then_inc(agg_step, 1)
            dve.wait_ge(agg_step, 2)
            nc.vector.tensor_copy(agg_parts[0:B, :], agg[:, :]).then_inc(agg_ok, 1)
            dve.wait_ge(agg_ok, 1)
            nc.vector.tensor_tensor(agg_parts[B:2 * B, :], agg[:, :], agg_parts[0:B, :].bitcast(F32), ALU.subtract).then_inc(agg_ok, 1)
            dve.wait_ge(att_mm, 1)
            nc.vector.tensor_copy(att_rows[:, :, :], att_rows_ps.rearrange("p (t k) -> p t k", t=NT)).then_inc(mix_step, 1)
            dve.wait_ge(mix_step, 1)
            dve.wait_ge(kernels_in, 16)

            nc.vector.tensor_tensor(mix_prod[:, 0:NH], att_rows[:, 0:NH, :].unsqueeze(2).broadcast_to([P, NH, C, KC]),
                                    kernels_sb[:, :, :].unsqueeze(1).broadcast_to([P, NH, C, KC]),
                                    ALU.mult).then_inc(mix_step, 1)
            dve.wait_ge(mix_step, 2)
            nc.vector.tensor_reduce(mix_rows[:, 0:NH, :], mix_prod[:, 0:NH], AX.X, ALU.add).then_inc(mix_step, 1)
            dve.wait_ge(mix_step, 3)
            nc.vector.tensor_tensor(mix[:, 0:NH], mix_rows[:, 0:NH, :].unsqueeze(3).broadcast_to([P, NH, C, BT]),
                                    cpart("own_block").unsqueeze(1).unsqueeze(1).broadcast_to([P, NH, C, BT]),
                                    ALU.mult).then_inc(mix_ok, 1)

            def bias_cond(t, u, slot_used):
                dve.wait_ge(cond_mm, t + 1)
                if slot_used:
                    dve.wait_ge(cond_hi, t - 1)
                bias = mix_bias[:, bass.ds(t, 1), :].broadcast_to([P, Q, P])
                nc.vector.tensor_tensor(cond32[:, u], cond_ps[u][:, :].rearrange("p (q n) -> p q n", q=Q),
                                        bias, ALU.add).then_inc(cond_biased, 1)

            def lo_of_cond(t, u, slot_used):
                dve.wait_ge(cond_hi, t + 1)
                if slot_used:
                    dve.wait_ge(y_mm, t - 1)
                nc.vector.tensor_tensor(cond_lo_sb[:, u], cond32[:, u], cond_hi_sb[:, u].bitcast(F32),
                                        ALU.subtract).then_inc(cond_lo, 1)

            def bias_y(t, u):
                dve.wait_ge(y_mm, t + 1)
                dve.wait_ge(gelus, t + 1)
                nc.vector.tensor_tensor(y32[:, u, :], y_ps[u][:, :], b2_sb[:, :], ALU.add).then_inc(s_then_y, 1)

            def residual(t, u):
                dve.wait_ge(gelus, t + 3)
                row = x1[:, bass.ds(t, 1), :].rearrange("p t l -> p (t l)")
                nc.vector.tensor_tensor(row, row, gelu_sb[:, u, :], ALU.add).then_inc(mix_then_x1, 1)

            def mask_chunk(q):
                dve.wait_ge(s_mm, q + 1)
                if q >= 2:
                    dve.wait_ge(s_hi_ok, q - 1)
                    dve.wait_ge(s_lo_ok, q - 1)
                nc.vector.tensor_tensor(s32[:, q % 2, :], s_ps[q][:, :], mask_sb[:, q, :], ALU.mult).then_inc(s_then_y, 1)

            def lo_of_s(q):
                dve.wait_ge(s_hi_ok, q + 1)
                nc.vector.tensor_tensor(s_lo[:, q, :], s32[:, q % 2, :], s_hi[:, q, :].bitcast(F32),
                                        ALU.subtract).then_inc(s_lo_ok, 1)

            dve.wait_ge(mask_in, 16)
            mask_chunk(0)
            lo_of_s(0)
            mask_chunk(1)
            dve.wait_ge(bias_ok, 2)
            bias_cond(0, 0, False)
            lo_of_s(1)
            lo_of_cond(0, 0, False)
            mask_chunk(2)
            bias_cond(1, 1, False)
            mask_chunk(3)
            lo_of_s(2)
            lo_of_s(3)
            lo_of_cond(1, 1, False)
            dve.wait_ge(b2_in, 16)
            dve.wait_ge(x1_in, 16)
            dve.wait_ge(mix_ok, 1)
            dve.wait_ge(mix_then_x1, 1)
            bias_y(0, 0)
            def step(k, u):
                bias_cond(k + 1, 1 - u, True)
                residual(k - 1, 1 - u)
                lo_of_cond(k + 1, 1 - u, True)
                bias_y(k, u)

            def main_lo_part(g, slot_used):
                dve.wait_ge(prep_hi, g * 3 + 1)
                if slot_used:
                    dve.wait_ge(conv_mm, g * 2)
                nc.vector.tensor_tensor(main_lo, main32[:, :, :], main_hi.bitcast(F32), ALU.subtract).then_inc(prep_lo, 1)

            def edge_lo_parts(g):
                dve.wait_ge(prep_lo, g * 3 + 1)
                nc.vector.tensor_copy(edge_view(2 * ER, 1), main_view(main_lo, P - ER, 0).bitcast(F32)).then_inc(prep_lo, 1)
                nc.vector.tensor_copy(edge_view(3 * ER, 0), main_view(main_lo, 0, 1).bitcast(F32)).then_inc(prep_lo, 1)

            with dve.Fori(0, NT // 2 - 2) as q:
                step(q * 2 + 1, 1)
                step(q * 2 + 2, 0)
            def z_parts(g, slot_used):
                for v in range(2):
                    dve.wait_ge(conv_mm, g * 2 + v + 1)
                    own = slice(2 * v, 2 * v + 2)
                    nc.vector.tensor_tensor(z_nat[:, own], z_ps[v][:, :].rearrange("p (g b m) -> p g b m", g=2, m=M),
                                            ctx_sb[:, own, bass.ds(g * BG, BG)].unsqueeze(3).broadcast_to([P, 2, BG, M]),
                                            ALU.add).then_inc(z_ok, 1)
                dve.wait_ge(z_ok, g * 2 + 2)
                if slot_used:
                    dve.wait_ge(z_hi, g * 2)
                for u in range(TG):
                    nc.vector.transpose(z32[:, :, u * P:(u + 1) * P].rearrange("p q (o c) -> p c q o", o=PG),
                                        z_nat[:, :, u * BT:(u + 1) * BT, :]).then_inc(zt_ok, 1)
                if slot_used:
                    dve.wait_ge(base_mm, g)
                for v in range(2):
                    own = slice(2 * v, 2 * v + 2)
                    dve.wait_ge(z_hi, g * 2 + v + 1)
                    nc.vector.tensor_tensor(z_lo_sb[:, own, :], z32[:, own, :], z_hi_sb[:, own, :].bitcast(F32), ALU.subtract).then_inc(z_lo, 1)
                dve.wait_ge(zt_ok, g * TG + TG)
                if slot_used:
                    dve.wait_ge(router_mm, g)
                nc.vector.tensor_reduce(zsum[:, :, :].rearrange("p q (u b) -> p (q u) b", u=TG),
                                        z32.rearrange("p q (u o b) -> p (q u) b o", u=TG, b=BT), AX.X, ALU.add).then_inc(zsum_ok, 1)

            def router(g):
                dve.wait_ge(router_mm, g + 1)
                nc.vector.tensor_reduce(router_max[:, :], router_ps[0:BG, 0:E], AX.X, ALU.max).then_inc(router_step, 1)
                dve.wait_ge(router_step, g * 3 + 1)
                nc.vector.tensor_scalar(router_bias[:, :], router_max[:, :], -ROUTER_SCALE, None, ALU.mult).then_inc(router_step, 1)
                dve.wait_ge(router_exp_ok, g + 1)
                nc.vector.reciprocal(router_inv[:, :], router_sum[:, :]).then_inc(router_step, 1)
                dve.wait_ge(router_step, g * 3 + 3)
                nc.vector.tensor_scalar(coef[:, :, :], router_exp[:, :].unsqueeze(2).broadcast_to([BG, E, RC]), router_inv[:, 0:1], None, ALU.mult).then_inc(coef_ok, 1)

            def h_parts(g, slot_used):
                dve.wait_ge(coef_mm, g + 1)
                nc.vector.tensor_copy(coef_rows[:, :, :], coef_ps.unsqueeze(1).broadcast_to([P, 2, BG])).then_inc(coef_rows_ok, 1)
                dve.wait_ge(coef_rows_ok, g + 1)
                for v in range(2):
                    dve.wait_ge(h_mm, g * 2 + v + 1)
                    if slot_used and v == 0:
                        dve.wait_ge(h_hi, g * 2)
                    nc.vector.tensor_tensor(h32[:, 2 * v:2 * v + 2].rearrange("p q (u o b) -> p (q u) o b", u=TG, b=BT),
                                            h_ps[v][:, :].rearrange("p (q o b) -> p q o b", o=C, b=BT),
                                            coef_rows[:, :, :].rearrange("p q (u b) -> p (q u) b", u=TG)
                                            .unsqueeze(2).broadcast_to([P, 2 * TG, C, BT]),
                                            ALU.mult).then_inc(h_ok, 1)
                for v in range(2):
                    dve.wait_ge(h_hi, g * 2 + v + 1)
                    if slot_used and v == 0:
                        dve.wait_ge(out_mm, g * TG)
                    nc.vector.tensor_tensor(h_lo_sb[:, 2 * v:2 * v + 2], h32[:, 2 * v:2 * v + 2],
                                            h_hi_sb[:, 2 * v:2 * v + 2].bitcast(F32), ALU.subtract).then_inc(h_lo, 1)

            def result(g):
                for u in range(TG):
                    dve.wait_ge(out_mm, g * TG + u + 1)
                    row = x1[:, bass.ds(g * TG + u, 1), :].rearrange("p t l -> p (t l)")
                    nc.vector.tensor_tensor(row, out_ps[u][:, :], row, ALU.add).then_inc(out_ok, 1)

            dve.wait_ge(x1_late_in, 16)
            k = NT - 3
            bias_cond(k + 1, 0, True)
            residual(k - 1, 0)
            lo_of_cond(k + 1, 0, True)
            main_lo_part(0, False)
            bias_y(k, 1)
            dve.wait_ge(zeros_ok, 1)
            edge_lo_parts(0)
            bias_cond(k + 2, 1, True)
            residual(k, 1)
            lo_of_cond(k + 2, 1, True)
            dve.wait_ge(ctx_ok, 1)
            dve.wait_ge(cond_lo, NT)
            z_parts(0, False)
            dve.wait_ge(keys_mm, 1)
            nc.vector.tensor_copy(folded_keys[:, :, :], keys_ps.rearrange("p (q e) -> p q e", q=Q)).then_inc(keys_ok, 1)
            bias_y(k + 1, 0)
            residual(k + 1, 0)
            bias_y(NT - 1, 1)
            residual(NT - 1, 1)
            router(0)
            main_lo_part(1, True)
            edge_lo_parts(1)
            h_parts(0, False)
            with dve.Fori(1, NG - 1) as g:
                z_parts(g, True)
                result(g - 1)
                router(g)
                main_lo_part(g + 1, True)
                edge_lo_parts(g + 1)
                h_parts(g, True)
            z_parts(NG - 1, True)
            result(NG - 2)
            router(NG - 1)
            h_parts(NG - 1, True)
            dve.wait_ge(out_mm, NT - 1)
            nc.vector.tensor_tensor(x1[:, NT - 2, :], out_ps[0][:, :], x1[:, NT - 2, :], ALU.add).then_inc(out_ok, 1)
            for v in range(2):
                dve.wait_ge(out_mm, NT + v)
                nc.vector.tensor_tensor(x1[:, NT - 1, half(v)], last_ps[v][:, half(v)],
                                        x1[:, NT - 1, half(v)], ALU.add).then_inc(out_ok, 1)

        @block.tensor
        def _(pe):
            def three(dst, lhs_hi, lhs_lo, rhs_hi, rhs_lo, first, last):
                pe.matmul(dst, lhs_hi, rhs_hi, start=first, stop=False)
                pe.matmul(dst, lhs_hi, rhs_lo, start=False, stop=False)
                return pe.matmul(dst, lhs_lo, rhs_hi, start=False, stop=last)

            def s_part(q, d):
                return three(s_ps[q][:, :], w1_hi[:, d, q * P:(q + 1) * P], w1_lo[:, d, q * P:(q + 1) * P],
                             w2_hi[:, d, :], w2_lo[:, d, :], d == 0, d == Q - 1)

            def s_wait(d):
                for s in (w1_hi_ok, w1_lo_ok, w2_hi_ok, w2_lo_ok):
                    pe.wait_ge(s, d + 1)

            def cond(t, u, bank_used):
                pe.wait_ge(x_slot_in[u], t * 8 - u * 8 + 16)
                if bank_used:
                    pe.wait_ge(cond_biased, t - 1)
                rhs = mix[:, bass.ds(t, 1)].rearrange("p t o b -> p (t o b)")
                for q in range(Q):
                    mm = pe.matmul(cond_ps[u][:, q * P:(q + 1) * P], x_slot[:, u, q * P:(q + 1) * P], rhs,
                                   start=True, stop=True)
                mm.then_inc(cond_mm, 1)

            def y(t, u, s_is_new=False):
                pe.wait_ge(cond_hi, t + 1)
                pe.wait_ge(cond_lo, t + 1)
                pe.wait_ge(s_then_y, t + Q - 1)
                for q in range(Q):
                    if s_is_new:
                        pe.wait_ge(s_hi_ok, q + 1)
                        pe.wait_ge(s_lo_ok, q + 1)
                    mm = three(y_ps[u][:, :], cond_hi_sb[:, u, q, :], cond_lo_sb[:, u, q, :], s_hi[:, q, :], s_lo[:, q, :],
                               q == 0, q == Q - 1)
                mm.then_inc(y_mm, 1)

            def keep_warm(n):
                for _ in range(n):
                    pe.matmul(s_ps[0][:, 0:P], ones[:, :], ones[:, :], start=True, stop=True)

            pe.wait_ge(ones_ok, 1)
            keep_warm(7)
            pe.wait_ge(small_in, 16)
            pe.matmul(h1_ps, part("w0"), part("emb_t"), start=True, stop=True).then_inc(mlp_mm, 1)
            keep_warm(2)
            pe.wait_ge(gelus, 1)
            pe.matmul(h2_ps, part("w1"), h1[:, :], start=True, stop=True).then_inc(mlp_mm, 1)
            def s_kind(lhs, rhs, q, first):
                pe.matmul(s_ps[q][:, :], lhs[:, 0, q * P:(q + 1) * P], rhs[:, 0, :], start=first, stop=False)

            pe.wait_ge(w1_hi_ok, 1)
            pe.wait_ge(w2_hi_ok, 1)
            for q in range(Q):
                s_kind(w1_hi, w2_hi, q, True)
                if q == 1:
                    pe.wait_ge(gelus, 2)
                    pe.matmul(logits_ps, h2[:, :], part("w2"), start=True, stop=True).then_inc(mlp_mm, 1)
            pe.wait_ge(w1_lo_ok, 1)
            for q in range(Q):
                s_kind(w1_lo, w2_hi, q, False)
            pe.wait_ge(w2_lo_ok, 1)
            for q in range(Q):
                s_kind(w1_hi, w2_lo, q, False)
            pe.wait_ge(ctx_terms, 1)
            for g in range(GROUPS):
                mm = pe.matmul(ctx_ps[:, g * B:(g + 1) * B], ctx_w_rep[:, g].rearrange("p r o -> p (r o)"), part("emb_t"),
                               start=True, stop=True)
            mm.then_inc(ctx_mm, 1)
            pe.wait_ge(soft, 6)
            pe.wait_ge(const_in, 16)
            pe.matmul(att_rows_ps, cpart("batch_rows", B), att_tiles[:, :, :].rearrange("b t k -> b (t k)"),
                      start=True, stop=True).then_inc(att_mm, 1)
            s_wait(1)
            for q in range(Q):
                s_part(q, 1)
            for q in range(Q):
                for d in range(2, Q):
                    if q == 0:
                        s_wait(d)
                    mm = s_part(q, d)
                mm.then_inc(s_mm, 1)
                if q == 0:
                    pe.wait_ge(bias_terms, 1)
                    pe.wait_ge(ones_r_ok, 1)
                    pe.wait_ge(mix_step, 1)
                    for v in range(2):
                        mm = pe.matmul(bias_ps[v][:, :], ones_r[:, :],
                                       bias_terms_sb[:, v * NT // 2:(v + 1) * NT // 2, :].rearrange("k t n -> k (t n)"),
                                       start=True, stop=True)
                    mm.then_inc(bias_mm, 1)
                    pe.wait_ge(mix_ok, 1)
                    pe.wait_ge(ctx_ok, 1)
                if 1 <= q <= 2:
                    cond(q - 1, q - 1, False)
            y(0, 0, True)
            pe.wait_ge(mix_then_x1, 1)
            with pe.Fori(0, NT // 2 - 1) as p:
                for k, u in ((p * 2 + 1, 1), (p * 2 + 2, 0)):
                    cond(k + 1, 1 - u, True)
                    y(k, u)

            def conv(g, bank_used):
                pe.wait_ge(prep_hi, g * 3 + 3)
                pe.wait_ge(prep_lo, g * 3 + 3)
                for v in range(2):
                    if bank_used:
                        pe.wait_ge(z_ok, g * 2 - 1 + v)
                    for grp in (2 * v, 2 * v + 1):
                        cols = slice(grp * P, (grp + 1) * P)
                        dst = z_ps[v][:, (grp % 2) * NTG:(grp % 2 + 1) * NTG].rearrange("p (u n) -> p u n", u=TG)
                        main_w, edge_w_hi, edge_w_lo = conv_hi[:, 0, cols], conv_hi[:, 1, cols], conv_lo[0:2 * ER, 1, cols]
                        pe.matmul(dst, main_w, main_hi[:, :, cols], start=True, stop=False)
                        pe.matmul(dst, main_w, main_lo[:, :, cols], start=False, stop=False)
                        pe.matmul(dst, conv_lo[:, 0, cols], main_hi[:, :, cols], start=False, stop=False)
                        pe.matmul(dst, edge_w_hi, edge[:, :, cols], start=False, stop=False)
                        mm = pe.matmul(dst, edge_w_lo, edge[0:2 * ER, :, cols], start=False, stop=True)
                    mm.then_inc(conv_mm, 1)

            def router_scores(g):
                pe.wait_ge(keys_ok, 1)
                pe.wait_ge(zsum_ok, g + 1)
                for q in range(Q):
                    mm = pe.matmul(router_ps[0:BG, 0:E], zsum[:, q, :], folded_keys[:, q, :], start=q == 0, stop=q == Q - 1)
                mm.then_inc(router_mm, 1)

            def h(g, bank_used):
                for c in range(Q):
                    if bank_used and c % 2 == 0:
                        pe.wait_ge(h_ok, g * 2 - 1 + c // 2)
                    dst = h_ps[c // 2][:, (c % 2) * NTG:(c % 2 + 1) * NTG]
                    cols = slice(c * P, (c + 1) * P)
                    for q in range(Q):
                        if c == 0 and q % 2 == 0:
                            pe.wait_ge(z_hi, g * 2 + q // 2 + 1)
                        pe.matmul(dst, down_hi[:, q, cols], z_hi_sb[:, q, :], start=q == 0, stop=False)
                        pe.matmul(dst, down_lo[:, q, cols], z_hi_sb[:, q, :], start=False, stop=False)
                    for q in range(Q):
                        if c == 0 and q % 2 == 0:
                            pe.wait_ge(z_lo, g * 2 + q // 2 + 1)
                        mm = pe.matmul(dst, down_hi[:, q, cols], z_lo_sb[:, q, :], start=False, stop=q == Q - 1)
                    if c % 2:
                        mm.then_inc(h_mm, 1)
                    if c == 1:
                        router_scores(g)

            def coef_on_rows(g):
                pe.wait_ge(coef_ok, g + 1)
                mm = pe.matmul(coef_ps, coef[:, :, :].rearrange("b e r -> b (e r)"), cpart("eye", BG)[:, 0:BG], start=True, stop=True)
                mm.then_inc(coef_mm, 1)

            def base(g, u, bank_used):
                if bank_used:
                    pe.wait_ge(out_ok, g * TG - TG + u + 1)
                rows = slice(u * P, (u + 1) * P)
                for q in range(Q):
                    mm = three(out_ps[u][:, :], z_hi_sb[:, q, rows], z_lo_sb[:, q, rows], ffn_hi[:, q, :], ffn_lo[:, q, :],
                               q == 0, False)
                if u == TG - 1:
                    mm.then_inc(base_mm, 1)

            def last_base(v):
                pe.wait_ge(z_ok, NG * 2)
                pe.wait_ge(out_ok, NT - TG)
                for q in range(Q):
                    three(last_ps[v][:, half(v)], z_hi_sb[:, q, P:2 * P], z_lo_sb[:, q, P:2 * P],
                          ffn_hi[:, q, half(v)], ffn_lo[:, q, half(v)], q == 0, False)

            def delta(g, tiles=TG):
                pe.wait_ge(h_hi, g * 2 + 2)
                pe.wait_ge(h_lo, g * 2 + 2)
                for u in range(tiles):
                    for c in range(Q):
                        rows = slice(u * P, (u + 1) * P)
                        mm = three(out_ps[u][:, :], h_hi_sb[:, c, rows], h_lo_sb[:, c, rows], up_hi[:, c, :], up_lo[:, c, :],
                                   False, c == Q - 1)
                    mm.then_inc(out_mm, 1)

            def last_delta():
                for v in range(2):
                    for c in range(Q):
                        mm = three(last_ps[v][:, half(v)], h_hi_sb[:, c, P:2 * P], h_lo_sb[:, c, P:2 * P],
                                   up_hi[:, c, half(v)], up_lo[:, c, half(v)], False, c == Q - 1)
                    mm.then_inc(out_mm, 1)

            pe.wait_ge(conv_w_ok, 2)
            pe.wait_ge(s_then_y, Q)
            conv(0, False)
            y(NT - 1, 1)
            pe.wait_ge(wq_in, 16)
            pe.wait_ge(bias_ok, 2)
            for q in range(Q):
                mm = pe.matmul(keys_ps[:, q * E:(q + 1) * E], wq_sb[:, q * P:(q + 1) * P], part("keys_t"), start=True, stop=True)
            mm.then_inc(keys_mm, 1)
            pe.wait_ge(down_ok, Q)
            h(0, False)
            pe.wait_ge(ffn_ok, Q)
            pe.wait_ge(s_then_y, Q + NT)
            base(0, 0, False)
            coef_on_rows(0)
            base(0, 1, False)
            conv(1, True)
            pe.wait_ge(up_ok, Q)
            delta(0)
            with pe.Fori(1, NG - 1) as g:
                h(g, True)
                base(g, 0, True)
                coef_on_rows(g)
                base(g, 1, True)
                conv(g + 1, True)
                delta(g)
            h(NG - 1, True)
            last_base(0)
            coef_on_rows(NG - 1)
            last_base(1)
            base(NG - 1, 0, True)
            delta(NG - 1, tiles=1)
            last_delta()


def kernel(**inputs):
    import numpy as np
    import concourse.bacc as bacc
    from concourse.bass_utils import run_bass_kernel_spmd

    a = {k: np.asarray(v) for k, v in inputs.items()}

    def phases(v):
        return np.ascontiguousarray(np.swapaxes(v.reshape(*v.shape[:-1], M, RP), -1, -2)).reshape(v.shape)

    def summed(v):
        w = v.reshape(*v.shape[:-1], M, RP // Q, Q)
        return np.ascontiguousarray(np.moveaxis(w, (-1, -2, -3), (-3, -2, -1))).reshape(v.shape)

    def tile_rows(v):
        w = v.reshape(NT, BT, GROUPS, PG, *v.shape[2:])
        return np.ascontiguousarray(np.moveaxis(w, (3, 2, 1), (1, 2, 3))).reshape(NT, P, *v.shape[2:])

    def channels(v, axis):
        w = v.reshape(*v.shape[:axis], GROUPS, PG, *v.shape[axis + 1:])
        return np.ascontiguousarray(np.swapaxes(w, axis, axis + 1)).reshape(v.shape)

    def chunks(v):
        return np.ascontiguousarray(v.reshape(Q, P, -1).transpose(1, 0, 2))

    def rows_of(v):
        full = np.zeros((P, v.shape[1]), v.dtype)
        full[:v.shape[0]] = v
        return full

    def repeat(v, rows=P):
        return np.repeat(v[None, :], rows, axis=0)

    f = np.float32
    small = {
        "emb_t": a["cond_128"].T, "w0": a["L0_cond_W0"], "b0": a["L0_cond_b0"][:, None], "w1": a["L0_cond_W1"],
        "b1": a["L0_cond_b1"][:, None], "w2": a["L0_cond_W2"], "b2": repeat(a["L0_cond_b2"]),
        "keys_t": a["L0_ffn_lora_keys"].T, "ctx_w_t": a["L0_cond2_c_weight"].T, "ctx_bias": np.tile(a["fside_S_0"].reshape(GROUPS, PG).T, (RP, 1)),
    }
    p, b = np.arange(P), np.arange(B)
    const = {
        "eye": rows_of(np.tile(np.eye(B, dtype=f), (2, 1))),
        "batch_rows": rows_of((b[:, None] % BT == p[None, :] % BT).astype(f)),
        "batch_tile": rows_of((b[:, None] // BT == np.arange(NT)[None, :]).astype(f)),
        "own_block": (p[:, None] % BT == np.arange(BT)[None, :]).astype(f),
    }
    taps = a["L0_cond2_weight"]
    conv_w = np.zeros((RP, PG, GROUPS, RP, PG), taps.dtype)
    sides = np.zeros((2, EDGE, PG, GROUPS, RP, PG), taps.dtype)
    for grp in range(GROUPS):
        own = taps[grp * PG:(grp + 1) * PG]
        for s in range(RP):
            for k in range(TAPS):
                r = s + k - PAD
                if r < 0:
                    sides[0, r + EDGE, :, grp, s] = own[:, :, k].T
                elif r >= RP:
                    sides[1, r - RP, :, grp, s] = own[:, :, k].T
                else:
                    conv_w[r, :, grp, s] = own[:, :, k].T
    sides = sides.reshape(2 * EDGE * PG, L)
    w2t = phases(np.ascontiguousarray(a["L0_attn_w2"].T))
    mask = phases(phases(a["L0_attn_sparse_mask"]).T.copy()).T
    ffn_w = phases(summed(a["L0_ffn_W_org"]).T.copy())

    def rank_rows(v):
        return np.ascontiguousarray(v.reshape(E, Q, RC, L).transpose(1, 0, 2, 3)).reshape(E * R, L)

    down = rank_rows(summed(a["L0_ffn_lora_down"].transpose(0, 2, 1))).T
    arrays = {
        "x": tile_rows(phases(a["x"])),
        "small": np.concatenate([small[n] for n, _ in _PACK], axis=1),
        "const": np.concatenate([const[n] for n, _ in _CONST], axis=1),
        "bias_k": repeat(channels(a["L0_cond_bias_k"], 1).T, B),
        "kernels_k": np.repeat(channels(channels(a["L0_cond_weight"][..., 0].transpose(2, 1, 0), 0), 1), BT, axis=0),
        "attn_w1": phases(a["L0_attn_w1"]).reshape(Q, P, L),
        "attn_w2t": w2t.reshape(Q, P, L),
        "mask": chunks(mask),
        "attn_b2": repeat(phases(a["L0_attn_b2"])),
        "wq": summed(a["L0_ffn_Wq"]),
        "conv_w": conv_w.reshape(P, L),
        "edge_w": np.concatenate([sides, sides], axis=0),
        "ffn_w": chunks(ffn_w),
        "lora_down": chunks(down),
        "lora_up": chunks(rank_rows(phases(a["L0_ffn_lora_up"]))),
    }
    arrays = {f"in_{k}": np.ascontiguousarray(v) for k, v in arrays.items()}
    nc = bacc.Bacc("TRN2", target_bir_lowering=False, num_devices=1)
    args = [nc.dram_tensor(k, v.shape, mybir.dt.from_np(v.dtype), kind="ExternalInput").ap() for k, v in arrays.items()]
    out = nc.dram_tensor("out", (NT, P, L), F32, kind="ExternalOutput").ap()
    adaln_attn_ffn(nc, *args, out)
    r = run_bass_kernel_spmd(nc, [arrays], core_ids=[0])
    got = r.results[0]["out"].reshape(NT, PG, GROUPS, BT, RP, M).transpose(0, 3, 2, 1, 5, 4)
    return np.ascontiguousarray(got).reshape(B, C, L)
```
